# Optimizing a Trainium2 kernel written in Bass

```python
import numpy as np
import jax
import jax.numpy as jnp

def _softmax(x, axis=-1):
    return jax.nn.softmax(x, axis=axis)

def _gelu(x):
    return jax.nn.gelu(x, approximate=True)

def _silu(x):
    return jax.nn.silu(x)

def _sigmoid(x):
    return jax.nn.sigmoid(x)

def _layernorm(x, axis=-1, eps=1e-05):
    m = jnp.mean(x, axis=axis, keepdims=True)
    v = jnp.var(x, axis=axis, keepdims=True)
    return (x - m) / jnp.sqrt(v + eps)

def _scatter_add(tgt, idx, src, axis=0):
    return tgt.at[idx].add(src)

def _segment_sum(src, seg, n):
    return jax.ops.segment_sum(src, seg, n)
kernel_name = 'mk_gnn_preln_d1_gnn_r64_18f078'

def setup_inputs(seed: int=0):
    np.random.seed(seed)
    _w = jnp.asarray

    def _rec_inputs():
        import jax
        import jax.numpy as jnp
        _gk = jax.random.key(seed)
        x = -0.0003713 + 1 * jax.random.normal(jax.random.fold_in(_gk, 1), (50000, 256), jnp.float32)
        src = jax.random.randint(jax.random.fold_in(_gk, 2), (12500,), 0, 50000, jnp.int32)
        dst = jnp.minimum((50000 * jax.random.uniform(jax.random.fold_in(_gk, 3), (12500,)) ** 2.0).astype(jnp.int32), 49999)
        _o = jnp.argsort(dst, stable=True)
        src = src[_o]
        dst = dst[_o]
        edge_attr_256 = 9.41057e-06 + 1 * jax.random.normal(jax.random.fold_in(_gk, 11), (12500, 256), jnp.float32)
        return (x, src, dst, edge_attr_256)
    x, src, dst, edge_attr_256 = _rec_inputs()

    def _L0_gnn_setup():
        import jax, jax.numpy as jnp
        import numpy as np
        N, E, NIN, H, C = (50000, 12500, 256, 8, 32)
        HC = H * C
        key = jax.random.key(seed)
        ks = jax.random.split(key, 12)
        s = 0.05
        x = jax.random.normal(ks[0], (N, NIN), dtype=jnp.float32)
        edge_index = jax.random.randint(ks[1], (2, E), 0, N, dtype=jnp.int64)
        edge_attr = jax.random.normal(ks[2], (E, NIN), dtype=jnp.float32)
        Wq = jax.random.normal(ks[3], (NIN, HC), dtype=jnp.float32) * s
        bq = jax.random.normal(ks[4], (HC,), dtype=jnp.float32) * s
        Wk = jax.random.normal(ks[5], (NIN, HC), dtype=jnp.float32) * s
        bk = jax.random.normal(ks[6], (HC,), dtype=jnp.float32) * s
        Wv = jax.random.normal(ks[7], (NIN, HC), dtype=jnp.float32) * s
        bv = jax.random.normal(ks[8], (HC,), dtype=jnp.float32) * s
        We = jax.random.normal(ks[9], (NIN, HC), dtype=jnp.float32) * s
        Ws = jax.random.normal(ks[10], (NIN, HC), dtype=jnp.float32) * s
        bs = jax.random.normal(ks[11], (HC,), dtype=jnp.float32) * s
        return {'x': x, 'edge_index': edge_index, 'edge_attr': edge_attr, 'Wq': Wq, 'bq': bq, 'Wk': Wk, 'bk': bk, 'Wv': Wv, 'bv': bv, 'We': We, 'Ws': Ws, 'bs': bs}
    _L0_gnn_all = _L0_gnn_setup()
    _L0_gnn_in = {k: v for k, v in _L0_gnn_all.items() if k in ('Wq', 'bq', 'Wk', 'bk', 'Wv', 'bv', 'We', 'Ws', 'bs')}
    del _L0_gnn_all
    return {'x': x, 'src': src, 'dst': dst, 'edge_attr_256': edge_attr_256, 'L0_gnn_Wq': _L0_gnn_in['Wq'], 'L0_gnn_bq': _L0_gnn_in['bq'], 'L0_gnn_Wk': _L0_gnn_in['Wk'], 'L0_gnn_bk': _L0_gnn_in['bk'], 'L0_gnn_Wv': _L0_gnn_in['Wv'], 'L0_gnn_bv': _L0_gnn_in['bv'], 'L0_gnn_We': _L0_gnn_in['We'], 'L0_gnn_Ws': _L0_gnn_in['Ws'], 'L0_gnn_bs': _L0_gnn_in['bs']}

def reference(x, src, dst, edge_attr_256, L0_gnn_Wq, L0_gnn_bq, L0_gnn_Wk, L0_gnn_bk, L0_gnn_Wv, L0_gnn_bv, L0_gnn_We, L0_gnn_Ws, L0_gnn_bs):
    import jax
    import jax.numpy as jnp

    def _L0_gnn_ref(x, edge_index, edge_attr, Wq, bq, Wk, bk, Wv, bv, We, Ws, bs):
        import jax, jax.numpy as jnp
        import numpy as np
        N, E, NIN, H, C = (50000, 12500, 256, 8, 32)
        HC = H * C
        src, dst = (edge_index[0], edge_index[1])
        n = x.shape[0]
        q = (x @ Wq + bq).reshape(n, H, C)
        k = (x @ Wk + bk).reshape(n, H, C)
        v = (x @ Wv + bv).reshape(n, H, C)
        e = (edge_attr @ We).reshape(-1, H, C)
        k_j = k[src] + e
        v_j = v[src] + e
        q_i = q[dst]
        alpha = jnp.sum(q_i * k_j, axis=-1) / jnp.sqrt(jnp.float32(C))
        amax = jax.ops.segment_max(alpha, dst, num_segments=n)
        ex = jnp.exp(alpha - amax[dst])
        denom = jax.ops.segment_sum(ex, dst, num_segments=n)
        alpha = ex / denom[dst]
        out = jax.ops.segment_sum(v_j * alpha[:, :, None], dst, num_segments=n)
        out = out.reshape(n, HC)
        out = out + x @ Ws + bs
        return out
    edge_index = jnp.stack([src, dst])
    h = jnp.maximum(_layernorm(x, axis=-1), 0.0)
    x = x + _L0_gnn_ref(h, edge_index, edge_attr_256, L0_gnn_Wq, L0_gnn_bq, L0_gnn_Wk, L0_gnn_bk, L0_gnn_Wv, L0_gnn_bv, L0_gnn_We, L0_gnn_Ws, L0_gnn_bs)
    return x

_drawn_inputs = setup_inputs


def setup_inputs(seed=0):
    import zlib

    import numpy as np

    out = dict(_drawn_inputs(seed))
    spreads = {}
    factors = {'L0_gnn_bq': 8.0, 'L0_gnn_Wk': 3.501, 'L0_gnn_bk': 8.0, 'L0_gnn_bv': 3.217}
    for name, (base, spread) in spreads.items():
        noise = np.random.default_rng([zlib.crc32(name.encode()), seed]).standard_normal(out[name].shape)
        drawn = base * np.exp(spread * noise) if base else spread * noise
        out[name] = jnp.asarray(drawn.astype(out[name].dtype))
    for name, factor in factors.items():
        out[name] = (out[name] * factor).astype(out[name].dtype)
    return out
```

```python
from contextlib import ExitStack

import concourse.bass as bass
from concourse import mybir

F32 = mybir.dt.float32
I32 = mybir.dt.int32
ALU = mybir.AluOpType
ACT = mybir.ActivationFunctionType
AX = mybir.AxisListType

P = 128


def build(nc, x, src, dst, edge_attr, Wq, bq, Wk, bk, Wv, bv, We, Ws, bs, out):
    N, D = x.shape
    E = src.shape[0]
    C = 32
    H = D // C
    KC = D // P
    HD = C + 1
    SCALE = float(C) ** -0.5
    EPS = 1e-5
    JT = 4
    GROUP = JT * P
    TILES = -(-E // P)
    FULL = N // GROUP
    REST = N - FULL * GROUP
    RJ = 3
    RP = REST // RJ
    assert FULL == TILES - 1 and RP * RJ == REST and RP <= P and TILES % 2 == 0
    LAST_EDGES = E - (TILES - 1) * P
    PADDED = TILES * P
    PAD_DST = 1 << 16
    SKIP = 1 << 17
    NEG = -3.0e38
    assert N < PAD_DST

    dst_table = nc.dram_tensor("dst_table", (PADDED + 2,), I32, kind="Internal").ap()
    src_table = nc.dram_tensor("src_table", (PADDED,), I32, kind="Internal").ap()
    edge_table = nc.dram_tensor("edge_table", (PADDED,), I32, kind="Internal").ap()

    ctx = ExitStack()
    with ctx:
        def sb(name, shape, dt=F32):
            return ctx.enter_context(nc.sbuf_tensor(name, shape, dt))

        def sem(name):
            return ctx.enter_context(nc.semaphore(name))

        def sem2(name):
            return [sem(f"{name}{u}") for u in range(2)]

        w_qs = sb("w_qs", [P, KC, 2 * D])
        w_kv = sb("w_kv", [P, KC, 2 * D])
        w_e = sb("w_e", [P, KC, D])
        bq_all = sb("bq_all", [P, D])
        bk_all = sb("bk_all", [P, D])
        bs_all = sb("bs_all", [P, D])
        bvs_all = sb("bvs_all", [P, D])
        ident = sb("ident", [P, P])
        minus_half = sb("minus_half", [P, JT + 2])
        last_row = sb("last_row", [P, 1])
        raw_dst = sb("raw_dst", [TILES, P], I32)
        raw_src = sb("raw_src", [TILES, P], I32)
        raw_edge = sb("raw_edge", [TILES, P], I32)
        ends = sb("ends", [1, 2], I32)
        table_i = sb("table_i", [TILES, 4, P], I32)
        table_f = sb("table_f", [TILES, 4, P])
        dst_col = sb("dst_col", [P, TILES + 1])
        same_next = sb("same_next", [P, TILES])
        dst_next = sb("dst_next", [P, TILES])
        gather_rows = sb("gather_rows", [P, TILES, 3], I32)
        scatter_rows = sb("scatter_rows", [P, TILES], I32)
        x_in = [sb(f"x_in{u}", [P, JT, D]) for u in range(2)]
        x_bs = [sb(f"x_bs{u}", [P, JT, D]) for u in range(2)]
        y_out = [sb(f"y_out{u}", [P, JT, D]) for u in range(2)]
        normed = [sb(f"normed{u}", [P, JT, D]) for u in range(2)]
        hT = [sb(f"hT{j}", [P, 2, KC, P]) for j in range(2)]
        rows_now = [sb(f"rows_now{u}", [P, 3], I32) for u in range(2)]
        x_src = [sb(f"x_src{u}", [P, D]) for u in range(2)]
        x_dst = [sb(f"x_dst{u}", [P, D]) for u in range(2)]
        e_in = [sb(f"e_in{u}", [P, D]) for u in range(2)]
        dst_row = [sb(f"dst_row{u}", [P, P + 2], I32) for u in range(2)]
        edge_normed = [sb(f"edge_normed{u}", [P, 2, D]) for u in range(2)]
        bn = sb("bn", [P, JT + 2, 6])
        stats = [sb(f"stats{u}", [P, JT + 2, 2]) for u in range(2)]
        var_eps = sb("var_eps", [P, JT + 2])
        rstd = [sb(f"rstd{u}", [P, JT + 2]) for u in range(2)]
        hT_edge = sb("hT_edge", [P, 2, KC, P])
        eT = sb("eT", [P, KC, P])
        x_dst_b = sb("x_dst_b", [P, D])
        e_sb = sb("e_sb", [P, D])
        e_bk = sb("e_bk", [P, D])
        q_sb = sb("q_sb", [P, D])
        k_sb = sb("k_sb", [P, D])
        qk = sb("qk", [P, D])
        v_sb = sb("v_sb", [P, D])
        alpha = sb("alpha", [P, H])
        break_prev = sb("break_prev", [H, P])
        break_next = sb("break_next", [H, P])
        neq_prev = sb("neq_prev", [H, P])
        neq_next = sb("neq_next", [H, P])
        run_max = [sb(f"run_max{u}", [H, P]) for u in range(2)]
        seg_max = sb("seg_max", [H, P])
        rise = sb("rise", [H, 1])
        below = sb("below", [P, H])
        weighted = sb("weighted", [P, H, HD])
        same = [sb(f"same{u}", [P, P]) for u in range(2)]
        carry_to = [sb(f"carry_to{u}", [P, P]) for u in range(2)]
        fade = sb("fade", [P, H])
        sums_sb = sb("sums_sb", [P, H, HD])
        carried = sb("carried", [P, H, HD])
        recip = sb("recip", [P, H])
        attn = sb("attn", [P, D])
        final = sb("final", [P, TILES, D])
        staged = x_bs

        def bank(name):
            return ctx.enter_context(nc.psum_tensor(name, [P, 512], F32))
        ps_hT_edge = bank("ps_hT_edge")
        ps_hT = bank("ps_hT")
        ps_y = [bank(f"ps_y{j}") for j in range(2)]
        ps_sums_bank = bank("ps_sums")
        ps_qs = bank("ps_qs")
        ps_kv = bank("ps_kv")
        ps_e = bank("ps_e")
        ps_sums = ps_sums_bank[:, 0:H * HD]
        ps_alphaT = ps_e[0:H, 0:P]
        ps_seg_max = ps_e[:, P:P + H]
        ps_rise = ps_e[:, P + H:P + 2 * H]
        ps_eT = ps_e[:, 0:D]
        ps_ev = ps_e[:, D:2 * D]
        ps_tab = ps_qs

        s_weights = sem("weights_loaded")
        s_bias = sem("biases_loaded")
        s_bvs = sem("bvs_ready")
        s_const = sem("const_ready")
        s_fill = sem("padding_filled")
        s_raw = sem("raw_indices_loaded")
        s_iota = sem("edge_numbers_ready")
        s_tables = sem("tables_written")
        s_tab_in = sem("tables_loaded")
        s_tab_f = sem("tables_float")
        s_tab_T = sem("tables_transposed")
        s_cols = sem("index_columns_ready")
        s_same_next = sem("same_next_ready")
        s_x = sem2("x_arrived")
        s_row = sem2("dst_row_arrived")
        s_gath = sem2("gathered")
        s_store = sem2("y_stored")
        s_rows_now = sem("rows_now_ready")
        s_bn = sem("bn_ready")
        s_stats = sem("stats_ready")
        s_var = sem("var_eps_ready")
        s_rstd = sem("rstd_ready")
        s_norm = sem("normed_ready")
        s_edgeT = sem("edge_rows_transposed")
        s_eT = sem("edge_attr_transposed")
        s_nodeT = sem("node_rows_transposed")
        s_hT_edge = sem("hT_edge_ready")
        s_eTs = sem("eT_ready")
        s_hT = sem("hT_ready")
        s_proj = sem("projected")
        s_mm = sem("node_products_done")
        s_xbs = sem("x_bs_ready")
        s_y = sem("y_ready")
        s_e = sem("e_ready")
        s_ebk = sem("e_bk_ready")
        s_xdb = sem("x_dst_b_ready")
        s_q = sem("q_ready")
        s_k = sem("k_ready")
        s_qk = sem("qk_ready")
        s_v = sem("v_ready")
        s_part = sem("final_part_ready")
        s_alpha = sem("alpha_ready")
        s_neq = sem("neq_ready")
        s_break = sem("breaks_ready")
        s_same = sem("same_ready")
        s_alphaT = sem("alpha_transposed")
        s_run = sem("run_max_ready")
        s_seg = sem("seg_max_ready")
        s_rise = sem("rise_ready")
        s_back = sem("seg_max_back")
        s_below = sem("below_ready")
        s_exp = sem("exp_ready")
        s_fade = sem("fade_ready")
        s_weighted = sem("weighted_ready")
        s_carried = sem("carried_ready")
        s_sums = sem("sums_done")
        s_sums_sb = sem("sums_sb_ready")
        s_recip = sem("recip_ready")
        s_attn = sem("attn_ready")
        s_final = sem("final_ready")
        s_staged = sem("staged_ready")
        s_scat = sem2("scattered")

        s_held = sem("waits_held")

        def nodes(n_is_last):
            return (RP, RJ) if n_is_last else (P, JT)

        def wait(eng, s, value):
            if isinstance(value, int) and value <= 0:
                return
            eng.wait_ge(s, value)

        def hold(eng):
            eng.sem_inc(s_held, 1)

        def loop(body, first_peeled=1, last_peeled=1):
            pairs = TILES // 2
            for i in range(first_peeled):
                for u in range(2):
                    body(2 * i + u, i, u)
            yield first_peeled, pairs - last_peeled
            for i in range(pairs - last_peeled, pairs):
                for u in range(2):
                    body(2 * i + u, i, u)

        def run(eng, body, first_peeled=1, last_peeled=1):
            for lo, hi in loop(body, first_peeled, last_peeled):
                with eng.Fori(lo, hi) as i:
                    for u in range(2):
                        body(i * 2 + u, i, u)

        x_groups = x[0:FULL * GROUP, :].rearrange("(g p j) d -> g p j d", p=P, j=JT)
        out_groups = out[0:FULL * GROUP, :].rearrange("(g p j) d -> g p j d", p=P, j=JT)
        x_rest = x[FULL * GROUP:N, :].rearrange("(p j) d -> p j d", j=RJ)
        out_rest = out[FULL * GROUP:N, :].rearrange("(p j) d -> p j d", j=RJ)

        block = ctx.enter_context(nc.Block())

        @block.sync
        def _(sp):
            def load_x(n, u):
                if isinstance(n, int) and n == FULL:
                    sp.dma_start(x_in[u][0:RP, 0:RJ, :], x_rest).then_inc(s_x[u], 16)
                else:
                    sp.dma_start(x_in[u][:, :, :], x_groups[n]).then_inc(s_x[u], 16)

            def load_row(n, u):
                sp.dma_start(dst_row[u][:, :], dst_table[bass.ds(n * P, P + 2)].partition_broadcast(P))\
                    .then_inc(s_row[u], 16)

            def store_y(n, u):
                if isinstance(n, int) and n == FULL:
                    sp.dma_start(out_rest, y_out[u][0:RP, 0:RJ, :]).then_inc(s_store[u], 16)
                else:
                    sp.dma_start(out_groups[n], y_out[u][:, :, :]).then_inc(s_store[u], 16)

            sp.wait_ge(s_fill, 3)
            full = (TILES - 1) * P
            for raw, given in ((raw_dst, dst), (raw_src, src)):
                sp.dma_start(raw[0:TILES - 1, :], given[0:full].rearrange("(t p) -> t p", p=P))\
                    .then_inc(s_raw, 16)
                sp.dma_start(raw[TILES - 1:TILES, 0:LAST_EDGES],
                             given[full:E].rearrange("(t p) -> t p", t=1)).then_inc(s_raw, 16)
            load_x(0, 0)
            load_x(1, 1)
            sp.wait_ge(s_raw, 64)
            sp.wait_ge(s_iota, 1)
            for table, raw in ((dst_table[1:PADDED + 1], raw_dst), (src_table, raw_src),
                               (edge_table, raw_edge)):
                sp.dma_start(table.rearrange("(t p) -> t p", p=P), raw[:, :]).then_inc(s_tables, 16)
            sp.dma_start(dst_table[0:1].rearrange("(t p) -> t p", t=1), ends[:, 0:1]).then_inc(s_tables, 16)
            sp.dma_start(dst_table[PADDED + 1:PADDED + 2].rearrange("(t p) -> t p", t=1), ends[:, 1:2])\
                .then_inc(s_tables, 16)
            sp.wait_ge(s_tables, 80)
            for k, table in enumerate((dst_table[1:PADDED + 1], dst_table[2:PADDED + 2], src_table,
                                       edge_table)):
                sp.dma_start(table_i[:, k, :], table.rearrange("(t p) -> t p", p=P)).then_inc(s_tab_in, 16)
            load_row(0, 0)
            load_row(1, 1)
            for c in range(KC):
                for w, given in ((w_e[:, c, :], We), (w_qs[:, c, 0:D], Wq), (w_qs[:, c, D:2 * D], Ws),
                                 (w_kv[:, c, 0:D], Wk), (w_kv[:, c, D:2 * D], Wv)):
                    sp.dma_start(w, given[c * P:(c + 1) * P, :]).then_inc(s_weights, 16)

            def step(n, i, u):
                last = isinstance(n, int) and n == FULL
                if not (isinstance(n, int) and n + 2 > FULL):
                    sp.wait_ge(s_norm, n * 3 + 3)
                    hold(sp)
                    sp.wait_ge(s_xbs, n + 1)
                    hold(sp)
                    load_x(n + 2, u)
                    sp.wait_ge(s_same, n + 1)
                    hold(sp)
                    load_row(n + 2, u)
                sp.wait_ge(s_y, n * 2 + 2)
                hold(sp)
                store_y(n, u)

            run(sp, step, first_peeled=0, last_peeled=2)
            for u in range(2):
                sp.wait_ge(s_store[u], 16 * (TILES // 2))

        @block.gpsimd
        def _(pool):
            pool.memset(raw_dst[:, :], PAD_DST).then_inc(s_fill, 1)
            pool.memset(raw_src[:, :], 0).then_inc(s_fill, 1)
            pool.memset(ends[:, :], -1).then_inc(s_fill, 1)
            pool.iota(raw_edge[:, :], pattern=[[1, P]], base=0, channel_multiplier=P).then_inc(s_iota, 1)
            pool.memset(ident[:, :], 0.0).then_inc(s_const, 1)
            pool.memset(last_row[:, :], 1.0).then_inc(s_const, 1)
            pool.memset(minus_half[:, :], -0.5).then_inc(s_const, 1)
            pool.memset(sums_sb[:, :, :], 0.0).then_inc(s_const, 1)
            pool.wait_ge(s_const, 4)
            pool.affine_select(out=ident[:, :], in_=ident[:, :], compare_op=ALU.not_equal, fill=1.0,
                               base=0, pattern=[[-1, P]], channel_multiplier=1).then_inc(s_const, 1)
            pool.affine_select(out=last_row[:, :], in_=last_row[:, :], compare_op=ALU.is_ge, fill=0.0,
                               base=-(P - 1), pattern=[[0, 1]], channel_multiplier=1).then_inc(s_const, 1)
            pool.wait_ge(s_bias, 80)
            pool.tensor_tensor(bvs_all[:, :], bvs_all[:, :], bs_all[:, :], ALU.add).then_inc(s_bvs, 1)
            pool.wait_ge(s_bvs, 1)

            def rstd_of(n, u):
                pool.wait_ge(s_stats, n + 1)
                hold(pool)
                pool.tensor_scalar(var_eps[:, :], stats[u][:, :, 1], EPS, None, ALU.add).then_inc(s_var, 1)
                pool.wait_ge(s_var, n + 1)
                pool.tensor_tensor(rstd[u][:, :], var_eps[:, :], minus_half[:, :], ALU.pow)\
                    .then_inc(s_rstd, 1)

            def gather(n, i, u):
                pool.tensor_copy(rows_now[u][:, :], gather_rows[:, n, :]).then_inc(s_rows_now, 1)
                pool.wait_ge(s_rows_now, n + 1)
                hold(pool)
                for k, (to, table, count) in enumerate(((x_src[u], x, N), (x_dst[u], x, N),
                                                        (e_in[u], edge_attr, E))):
                    pool.indirect_dma_start(
                        out=to[:, :], out_offset=None, in_=table[:, :],
                        in_offset=bass.IndirectOffsetOnAxis(ap=rows_now[u][:, k:k + 1], axis=0),
                        bounds_check=count - 1, oob_is_err=False).then_inc(s_gath[u], 16)

            def x_and_bias(n, i, u):
                p, j = nodes(isinstance(n, int) and n == FULL)
                pool.wait_ge(s_x[u], i * 16 + 16)
                wait(pool, s_y, n * 2 - 2)
                pool.tensor_tensor(x_bs[u][0:p, 0:j, :], x_in[u][0:p, 0:j, :],
                                   bs_all[0:p, :].unsqueeze(1).to_broadcast([p, j, D]), ALU.add)\
                    .then_inc(s_xbs, 1)

            def carry(m, u):
                pool.wait_ge(s_fade, m + 1)
                wait(pool, s_sums_sb, m)
                pool.tensor_tensor(carried[:, :, :], sums_sb[:, :, :],
                                   fade[:, :].unsqueeze(2).to_broadcast([P, H, HD]), ALU.mult)\
                    .then_inc(s_carried, 1)

            def finish(m):
                pool.wait_ge(s_attn, m + 1)
                pool.wait_ge(s_part, m + 1)
                pool.tensor_tensor(final[:, m, :], final[:, m, :], attn[:, :], ALU.add).then_inc(s_final, 1)

            def step(n, i, u):
                first = isinstance(n, int) and n == 0
                last = isinstance(n, int) and n == TILES - 1
                if not first:
                    carry(n - 1, 1 - u)
                if not last:
                    rstd_of(n + 1, 1 - u)
                pool.wait_ge(s_gath[u], i * 48 + 48)
                wait(pool, s_part, n)
                pool.tensor_tensor(x_dst_b[:, :], x_dst[u][:, :], bvs_all[:, :], ALU.add)\
                    .then_inc(s_xdb, 1)
                x_and_bias(n, i, u)
                pool.wait_ge(s_e, n + 1)
                wait(pool, s_k, n)
                pool.tensor_tensor(e_bk[:, :], e_sb[:, :], bk_all[:, :], ALU.add).then_inc(s_ebk, 1)
                if not (isinstance(n, int) and n + 2 > TILES - 1):
                    pool.wait_ge(s_norm, n * 3 + 1)
                    pool.wait_ge(s_eT, n + 1)
                    pool.wait_ge(s_xdb, n + 1)
                    gather(n + 2, i + 1, u)
                if not first:
                    finish(n - 1)

            pool.wait_ge(s_cols, 3)
            gather(0, 0, 0)
            gather(1, 0, 1)
            rstd_of(0, 0)
            run(pool, step)
            carry(TILES - 1, 1)
            finish(TILES - 1)

            for u in range(2):
                pool.wait_ge(s_store[u], 16 * (TILES // 2))
            with pool.Fori(0, TILES // 2) as i:
                for u in range(2):
                    pool.wait_ge(s_staged, i * 2 + u + 1)
                    hold(pool)
                    pool.indirect_dma_start(
                        out=out[:, :],
                        out_offset=bass.IndirectOffsetOnAxis(ap=rows_now[u][:, 0:1], axis=0),
                        in_=staged[u][:, 0, :], in_offset=None,
                        bounds_check=N - 1, oob_is_err=False).then_inc(s_scat[u], 16)
            for u in range(2):
                pool.wait_ge(s_scat[u], 16 * (TILES // 2))

        @block.scalar
        def _(act):
            for b, given in ((bq_all, bq), (bk_all, bk), (bs_all, bs), (bvs_all, bv)):
                act.dma_start(b[:, :], given.partition_broadcast(P)).then_inc(s_bias, 16)
            act.dma_start(dst_next[0:1, 0:1], bs[0:1].rearrange("(a b) -> a b", a=1)).then_inc(s_bias, 16)

            def exps(m, u):
                act.wait_ge(s_below, m + 1)
                act.activation(weighted[:, :, C], below[:, :], ACT.Exp, scale=SCALE).then_inc(s_exp, 1)
                act.wait_ge(s_back, m + 1)
                act.activation(fade[:, :], ps_rise, ACT.Exp, scale=-SCALE).then_inc(s_fade, 1)

            def node_hT(n, j):
                act.wait_ge(s_nodeT, n * 2 + j + 1)
                wait(act, s_mm, n * 2 + j - 1)
                p, tiles = nodes(isinstance(n, int) and n == FULL)
                count = min(2, tiles - 2 * j)
                act.activation(hT[j][:, 0:count, :, 0:p],
                               ps_hT[:, :].rearrange("a (t c p) -> a t c p", t=2, c=KC)[:, 0:count, :, 0:p],
                               ACT.Relu).then_inc(s_hT, 1)

            def keep_sums(m):
                act.wait_ge(s_sums, m + 1)
                wait(act, s_attn, m)
                act.activation(sums_sb[:, :, :], ps_sums.rearrange("p (h c) -> p h c", c=HD),
                               ACT.Copy).then_inc(s_sums_sb, 1)

            def step(n, i, u):
                first = isinstance(n, int) and n == 0
                act.wait_ge(s_edgeT, n + 1)
                wait(act, s_proj, n * 3)
                act.activation(hT_edge[:, :, :, :],
                               ps_hT_edge[:, :].rearrange("a (t c p) -> a t c p", t=2, c=KC),
                               ACT.Relu).then_inc(s_hT_edge, 1)
                if not first:
                    exps(n - 1, 1 - u)
                node_hT(n, 0)
                act.wait_ge(s_eT, n + 1)
                act.activation(eT[:, :, :], ps_eT.rearrange("a (c p) -> a c p", c=KC), ACT.Copy)\
                    .then_inc(s_eTs, 1)
                act.wait_ge(s_proj, n * 3 + 2)
                wait(act, s_v, n)
                wait(act, s_ebk, n)
                act.activation(e_sb[:, :], ps_ev, ACT.Copy).then_inc(s_e, 1)
                node_hT(n, 1)
                if not first:
                    keep_sums(n - 1)

            run(act, step)
            exps(TILES - 1, 1)
            keep_sums(TILES - 1)

            act.wait_ge(s_final, TILES)
            for u in range(2):
                act.wait_ge(s_store[u], 16 * (TILES // 2))
            def stage(t, i, u):
                if not (isinstance(t, int) and t < 2):
                    act.wait_ge(s_scat[u], i * 16)
                act.activation(staged[u][:, 0, :], final[:, t, :], ACT.Copy)
                act.copy(rows_now[u][:, 0:1], scatter_rows[:, bass.ds(t, 1)]).then_inc(s_staged, 1)
            run(act, stage, first_peeled=1, last_peeled=0)

        @block.vector
        def _(dve):
            dve.wait_ge(s_tab_in, 64)
            dve.tensor_copy(table_f[:, :, :], table_i[:, :, :]).then_inc(s_tab_f, 1)
            dve.wait_ge(s_tab_T, 1)
            dve.wait_ge(s_bias, 80)
            cols = ps_tab[:, 0:4 * TILES].rearrange("p (k t) -> p k t", k=4)
            dve.memset(dst_col[:, 0:1], -1.0)
            dve.tensor_copy(dst_col[:, 1:TILES + 1], cols[:, 0, :]).then_inc(s_same_next, 1)
            dve.tensor_copy(dst_next[:, :], cols[:, 1, :]).then_inc(s_same_next, 1)
            dve.tensor_copy(gather_rows[:, :, 0], cols[:, 2, :]).then_inc(s_cols, 1)
            dve.tensor_scalar(gather_rows[:, :, 1], cols[:, 0, :], float(N - 1), None, ALU.min)\
                .then_inc(s_cols, 1)
            dve.tensor_scalar(gather_rows[:, :, 2], cols[:, 3, :], float(E - 1), None, ALU.min)\
                .then_inc(s_cols, 1)
            dve.wait_ge(s_same_next, 2)
            dve.tensor_tensor(same_next[:, :], dst_col[:, 1:TILES + 1], dst_next[:, :], ALU.is_equal)\
                .then_inc(s_same_next, 1)
            dve.wait_ge(s_same_next, 3)
            dve.scalar_tensor_tensor(out=scatter_rows[:, :], in0=same_next[:, :], scalar=float(SKIP),
                                     in1=dst_col[:, 1:TILES + 1], op0=ALU.mult, op1=ALU.add)\
                .then_inc(s_cols, 1)

            def statistics(n, i, u):
                p, tiles = nodes(isinstance(n, int) and n == FULL)
                dve.wait_ge(s_gath[u], i * 48 + 48)
                dve.wait_ge(s_x[u], i * 16 + 16)
                dve.bn_stats(bn[:, 0, :], x_src[u][:, :])
                done = dve.bn_stats(bn[:, 1, :], x_dst[u][:, :])
                for j in range(tiles):
                    done = dve.bn_stats(bn[0:p, 2 + j, :], x_in[u][0:p, j, :])
                done.then_inc(s_bn, 1)
                dve.wait_ge(s_bn, n + 1)
                hold(dve)
                for j in range(JT + 2):
                    done = dve.bn_aggr(stats[u][:, j, :], bn[:, j, :])
                done.then_inc(s_stats, 1)

            def normalise(n, i, u):
                p, tiles = nodes(isinstance(n, int) and n == FULL)
                dve.wait_ge(s_rstd, n + 1)
                wait(dve, s_edgeT, n - 1)
                for k, rows in enumerate((x_src[u], x_dst[u])):
                    done = dve.tensor_scalar(edge_normed[u][:, k, :], rows[:, :], stats[u][:, k, 0:1],
                                             rstd[u][:, k:k + 1], ALU.subtract, ALU.mult)
                done.then_inc(s_norm, 1)
                wait(dve, s_nodeT, n * 2 - 2)
                for j in range(JT):
                    if j < tiles:
                        done = dve.tensor_scalar(normed[u][0:p, j, :], x_in[u][0:p, j, :],
                                                 stats[u][0:p, 2 + j, 0:1], rstd[u][0:p, 2 + j:3 + j],
                                                 ALU.subtract, ALU.mult)
                    if j % 2:
                        done.then_inc(s_norm, 1)

            def y_add(n, i, u, j):
                p, tiles = nodes(isinstance(n, int) and n == FULL)
                count = min(2, tiles - 2 * j)
                dve.wait_ge(s_mm, n * 2 + j + 1)
                if j == 0:
                    dve.wait_ge(s_xbs, n + 1)
                    if not (isinstance(i, int) and i == 0):
                        dve.wait_ge(s_store[u], i * 16)
                dve.tensor_tensor(y_out[u][0:p, 2 * j:2 * j + count, :],
                                  ps_y[j][0:p, 0:count * D].rearrange("p (t d) -> p t d", d=D),
                                  x_bs[u][0:p, 2 * j:2 * j + count, :], ALU.add).then_inc(s_y, 1)

            def head_dim(ap):
                return ap.rearrange("p (h c) -> p h c", c=C)

            def scores(n, i, u):
                dve.wait_ge(s_proj, n * 3 + 1)
                dve.tensor_tensor(q_sb[:, :], ps_qs[:, 0:D], bq_all[:, :], ALU.add).then_inc(s_q, 1)
                dve.wait_ge(s_xdb, n + 1)
                dve.tensor_tensor(final[:, n, :], ps_qs[:, D:2 * D], x_dst_b[:, :], ALU.add)\
                    .then_inc(s_part, 1)
                dve.wait_ge(s_proj, n * 3 + 3)
                dve.wait_ge(s_ebk, n + 1)
                dve.tensor_tensor(k_sb[:, :], ps_kv[:, 0:D], e_bk[:, :], ALU.add).then_inc(s_k, 1)
                dve.wait_ge(s_q, n + 1)
                dve.wait_ge(s_k, n + 1)
                dve.tensor_tensor(qk[:, :], q_sb[:, :], k_sb[:, :], ALU.mult).then_inc(s_qk, 1)
                dve.wait_ge(s_e, n + 1)
                dve.tensor_tensor(v_sb[:, :], ps_kv[:, D:2 * D], e_sb[:, :], ALU.add).then_inc(s_v, 1)
                dve.wait_ge(s_qk, n + 1)
                dve.tensor_reduce(out=alpha[:, :], in_=head_dim(qk[:, :]), op=ALU.add, axis=AX.X)\
                    .then_inc(s_alpha, 1)

            def segments(n, i, u):
                dve.wait_ge(s_row[u], i * 16 + 16)
                row = dst_row[u]
                dve.tensor_tensor(neq_prev[:, :], row[0:H, 1:P + 1], row[0:H, 0:P], ALU.not_equal)
                dve.tensor_tensor(neq_next[:, :], row[0:H, 1:P + 1], row[0:H, 2:P + 2], ALU.not_equal)\
                    .then_inc(s_neq, 1)
                dve.tensor_scalar(carry_to[u][96:P, :], row[96:P, 1:P + 1], dst_col[96:P, bass.ds(n, 1)],
                                  last_row[96:P, :], ALU.is_equal, ALU.mult)
                dve.tensor_scalar(same[u][:, :], row[:, 1:P + 1], dst_col[:, bass.ds(n + 1, 1)], None,
                                  ALU.is_equal).then_inc(s_same, 1)
                dve.wait_ge(s_neq, n + 1)
                dve.tensor_scalar(break_prev[:, :], neq_prev[:, :], NEG, None, ALU.mult)
                dve.tensor_scalar(break_next[:, :], neq_next[:, :], NEG, None, ALU.mult)\
                    .then_inc(s_break, 1)

            def maxima(n, i, u):
                first = isinstance(n, int) and n == 0
                dve.wait_ge(s_break, n + 1)
                dve.wait_ge(s_alphaT, n + 1)
                before = 0.0 if first else run_max[1 - u][:, P - 1:P]
                dve.tensor_tensor_scan(run_max[u][:, :], break_prev[:, :], ps_alphaT, before,
                                       ALU.add, ALU.max).then_inc(s_run, 1)
                dve.wait_ge(s_run, n + 1)
                dve.tensor_tensor_scan(seg_max[:, ::-1], break_next[:, ::-1], run_max[u][:, ::-1], NEG,
                                       ALU.add, ALU.max).then_inc(s_seg, 1)
                dve.wait_ge(s_seg, n + 1)
                dve.tensor_scalar(rise[:, :], seg_max[:, 0:1], before, 0.0, ALU.subtract, ALU.max)\
                    .then_inc(s_rise, 1)

            def weigh(m):
                dve.wait_ge(s_exp, m + 1)
                dve.wait_ge(s_v, m + 1)
                dve.tensor_tensor(weighted[:, :, 0:C], head_dim(v_sb[:, :]),
                                  weighted[:, :, C:HD].to_broadcast([P, H, C]), ALU.mult)\
                    .then_inc(s_weighted, 1)

            def divide(m):
                sums = sums_sb[:, :, :]
                dve.wait_ge(s_sums_sb, m + 1)
                dve.reciprocal(recip[:, :], sums[:, :, C]).then_inc(s_recip, 1)
                dve.wait_ge(s_recip, m + 1)
                wait(dve, s_final, m)
                dve.tensor_tensor(head_dim(attn[:, :]), sums[:, :, 0:C],
                                  recip[:, :].unsqueeze(2).to_broadcast([P, H, C]), ALU.mult)\
                    .then_inc(s_attn, 1)

            def step(n, i, u):
                first = isinstance(n, int) and n == 0
                last = isinstance(n, int) and n == TILES - 1
                back = i if u else i - 1
                ahead = i + 1 if u else i
                if not first:
                    dve.wait_ge(s_back, n)
                    dve.tensor_tensor(below[:, :], alpha[:, :], ps_seg_max, ALU.subtract)\
                        .then_inc(s_below, 1)
                    y_add(n - 1, back, 1 - u, 1)
                if not last:
                    statistics(n + 1, ahead, 1 - u)
                if not first:
                    weigh(n - 1)
                if not last:
                    normalise(n + 1, ahead, 1 - u)
                scores(n, i, u)
                segments(n, i, u)
                y_add(n, i, u, 0)
                maxima(n, i, u)
                if not first:
                    divide(n - 1)

            statistics(0, 0, 0)
            normalise(0, 0, 0)
            run(dve, step)
            m = TILES - 1
            dve.wait_ge(s_back, m + 1)
            dve.tensor_tensor(below[:, :], alpha[:, :], ps_seg_max, ALU.subtract).then_inc(s_below, 1)
            y_add(m, TILES // 2 - 1, 1, 1)
            weigh(m)
            divide(m)

        @block.tensor
        def _(pe):
            pe.wait_ge(s_const, 6)
            pe.wait_ge(s_tab_f, 1)
            for k in range(4):
                done = pe.transpose(ps_tab[:, k * TILES:(k + 1) * TILES], table_f[:, k, :],
                                    ident[0:TILES, 0:TILES])
            done.then_inc(s_tab_T, 1)
            pe.wait_ge(s_weights, 16 * 5 * KC)
            pe.wait_ge(s_cols, 4)

            def chunk(c):
                return slice(c * P, (c + 1) * P)

            def edge_transposes(n, i, u):
                pe.wait_ge(s_norm, n * 3 + 1)
                wait(pe, s_hT_edge, n)
                for k in range(2):
                    for c in range(KC):
                        at = (k * KC + c) * P
                        done = pe.transpose(ps_hT_edge[:, at:at + P], edge_normed[u][:, k, chunk(c)],
                                            ident[:, :])
                done.then_inc(s_edgeT, 1)

            def attr_transposes(n, i, u):
                pe.wait_ge(s_gath[u], i * 48 + 48)
                wait(pe, s_below, n)
                wait(pe, s_fade, n)
                for c in range(KC):
                    done = pe.transpose(ps_eT[:, c * P:(c + 1) * P], e_in[u][:, chunk(c)], ident[:, :])
                done.then_inc(s_eT, 1)

            def node_transposes(n, i, u, j):
                p, tiles = nodes(isinstance(n, int) and n == FULL)
                pe.wait_ge(s_norm, n * 3 + 2 + j)
                wait(pe, s_hT, n * 2 + j)
                for k in range(min(2, tiles - 2 * j)):
                    for c in range(KC):
                        at = (k * KC + c) * P
                        done = pe.transpose(ps_hT[:, at:at + p], normed[u][0:p, 2 * j + k, chunk(c)],
                                            ident[0:p, 0:p])
                done.then_inc(s_nodeT, 1)

            def node_products(n, i, u, j):
                p, tiles = nodes(isinstance(n, int) and n == FULL)
                pe.wait_ge(s_hT, n * 2 + j + 1)
                wait(pe, s_y, n * 2 + j - 1)
                for k in range(min(2, tiles - 2 * j)):
                    for c in range(KC):
                        done = pe.matmul(ps_y[j][0:p, k * D:(k + 1) * D], hT[j][:, k, c, 0:p],
                                         w_qs[:, c, D:2 * D], start=c == 0, stop=c == KC - 1)
                done.then_inc(s_mm, 1)

            def projections(n, i, u):
                pe.wait_ge(s_hT_edge, n + 1)
                wait(pe, s_part, n)
                for c in range(KC):
                    done = pe.matmul(ps_qs[:, :], hT_edge[:, 1, c, :], w_qs[:, c, :],
                                     start=c == 0, stop=c == KC - 1)
                done.then_inc(s_proj, 1)
                pe.wait_ge(s_eTs, n + 1)
                for c in range(KC):
                    done = pe.matmul(ps_ev, eT[:, c, :], w_e[:, c, :], start=c == 0, stop=c == KC - 1)
                done.then_inc(s_proj, 1)
                wait(pe, s_v, n)
                for c in range(KC):
                    done = pe.matmul(ps_kv[:, :], hT_edge[:, 0, c, :], w_kv[:, c, :],
                                     start=c == 0, stop=c == KC - 1)
                done.then_inc(s_proj, 1)

            def segment_sums(m, u):
                pe.wait_ge(s_weighted, m + 1)
                pe.wait_ge(s_carried, m + 1)
                pe.wait_ge(s_same, m + 1)
                wait(pe, s_sums_sb, m)
                flat = "p h c -> p (h c)"
                pe.matmul(ps_sums, same[u][:, :], weighted[:, :, :].rearrange(flat), start=True, stop=False)
                pe.matmul(ps_sums, carry_to[u][96:P, :], carried[96:P, :, :].rearrange(flat),
                          start=False, stop=True).then_inc(s_sums, 1)

            def step(n, i, u):
                first = isinstance(n, int) and n == 0
                edge_transposes(n, i, u)
                node_transposes(n, i, u, 0)
                attr_transposes(n, i, u)
                projections(n, i, u)
                node_transposes(n, i, u, 1)
                node_products(n, i, u, 0)
                if not first:
                    segment_sums(n - 1, 1 - u)
                pe.wait_ge(s_e, n + 1)
                pe.wait_ge(s_alpha, n + 1)
                pe.transpose(ps_alphaT, alpha[:, :], ident[:, :]).then_inc(s_alphaT, 1)
                node_products(n, i, u, 1)
                pe.wait_ge(s_rise, n + 1)
                hold(pe)
                pe.transpose(ps_seg_max, seg_max[:, :], ident[0:H, 0:H])
                pe.matmul(ps_rise, rise[:, 0:1].to_broadcast([H, P]), ident[0:H, 0:H],
                          start=True, stop=True).then_inc(s_back, 1)

            run(pe, step)
            segment_sums(TILES - 1, 1)


_INS = ["x", "src", "dst", "edge_attr_256", "L0_gnn_Wq", "L0_gnn_bq", "L0_gnn_Wk", "L0_gnn_bk",
        "L0_gnn_Wv", "L0_gnn_bv", "L0_gnn_We", "L0_gnn_Ws", "L0_gnn_bs"]


def kernel(**inputs):
    import numpy as _np
    import concourse.bacc as _bacc
    from concourse import mybir as _mybir
    from concourse.bass_utils import run_bass_kernel_spmd as _run

    nc = _bacc.Bacc("TRN2", target_bir_lowering=False, num_devices=1)
    arrays, args = {}, []
    for name in _INS:
        a = _np.ascontiguousarray(inputs[name])
        arrays[f"in_{name}"] = a
        args.append(nc.dram_tensor(f"in_{name}", a.shape, _mybir.dt.from_np(a.dtype), kind="ExternalInput").ap())
    args.append(nc.dram_tensor("out_rows", inputs["x"].shape, _mybir.dt.float32, kind="ExternalOutput").ap())
    build(nc, *args)
    r = _run(nc, [arrays], core_ids=[0])
    return r.results[0]["out_rows"]
```

```python
from contextlib import ExitStack

import concourse.bass as bass
from concourse import mybir

F32 = mybir.dt.float32
I32 = mybir.dt.int32
BF16 = mybir.dt.bfloat16
I16 = mybir.dt.int16
ALU = mybir.AluOpType
ACT = mybir.ActivationFunctionType
AX = mybir.AxisListType

P = 128


def build(nc, x, src, dst, edge_attr, Wq, bq, Wk, bk, Wv, bv, We, Ws, bs, out):
    N, D = x.shape
    E = src.shape[0]
    C = 32
    H = D // C
    KC = D // P
    HD = C + 1
    SCALE = float(C) ** -0.5
    EPS = 1e-5
    JT = 4
    GROUP = JT * P
    TILES = -(-E // P)
    FULL = N // GROUP
    REST = N - FULL * GROUP
    RJ = 3
    RP = REST // RJ
    assert FULL == TILES - 1 and RP * RJ == REST and RP <= P and TILES % 2 == 0
    LAST_EDGES = E - (TILES - 1) * P
    PADDED = TILES * P
    PAD_DST = 1 << 16
    SKIP = 1 << 17
    NEG = -3.0e38
    APART = 2.0 ** 110
    assert N < PAD_DST

    dst_table = nc.dram_tensor("dst_table", (PADDED + 2,), F32, kind="Internal").ap()
    src_table = nc.dram_tensor("src_table", (PADDED + 2,), I32, kind="Internal").ap()
    edge_table = nc.dram_tensor("edge_table", (PADDED + 2,), I32, kind="Internal").ap()

    ctx = ExitStack()
    with ctx:
        def sb(name, shape, dt=F32):
            return ctx.enter_context(nc.sbuf_tensor(name, shape, dt))

        def sem(name):
            return ctx.enter_context(nc.semaphore(name))

        def sem2(name):
            return [sem(f"{name}{u}") for u in range(2)]

        w_qs = sb("w_qs", [P, KC, 2 * D])
        w_kv = sb("w_kv", [P, KC, 2 * D])
        w_e = sb("w_e", [P, KC, D])
        ones3 = sb("ones3", [3, P], BF16)
        bias_row = sb("bias_row", [1, 2 * D])
        bias_part = [sb(f"bias_part{k}", [1, 2 * D], BF16) for k in range(3)]
        bias3 = sb("bias3", [3, 2 * D], BF16)
        bs_all = sb("bs_all", [P, D])
        bvs_all = sb("bvs_all", [P, D])
        ident = sb("ident", [P, P])
        minus_half = sb("minus_half", [P, JT + 2])
        last_row = sb("last_row", [P, 1])
        raw_dst = sb("raw_dst", [TILES, P], I32)
        raw_src = sb("raw_src", [TILES, P], I32)
        raw_edge = sb("raw_edge", [TILES, P], I32)
        raw_next = sb("raw_next", [TILES, P], I32)
        falls = sb("falls", [TILES, P])
        row_falls = sb("row_falls", [TILES, 1])
        unsorted = sb("unsorted", [1, 1], I32)
        key_col = sb("key_col", [P, TILES])
        src_col = sb("src_col", [P, TILES], I32)
        edge_col = sb("edge_col", [P, TILES], I32)
        count = sb("count", [P, 1])
        place = sb("place", [P, 1], I32)
        moved_dst = sb("moved_dst", [P, 1])
        moved_src = sb("moved_src", [P, 1], I32)
        moved_edge = sb("moved_edge", [P, 1], I32)
        ends = sb("ends", [1, 2])
        scaled_dst = sb("scaled_dst", [TILES, P])
        table_i = sb("table_i", [TILES, 2, P], I32)
        table_f = sb("table_f", [TILES, 4, P])
        dst_col = sb("dst_col", [P, TILES + 1])
        same_next = sb("same_next", [P, TILES])
        dst_next = sb("dst_next", [P, TILES])
        gather_rows = sb("gather_rows", [P, TILES, 3], I32)
        scatter_rows = sb("scatter_rows", [P, TILES], I32)
        x_in = [sb(f"x_in{u}", [P, JT, D]) for u in range(2)]
        x_bs = [sb(f"x_bs{u}", [P, JT, D]) for u in range(2)]
        y_out = [sb(f"y_out{u}", [P, JT, D]) for u in range(2)]
        normed = [sb(f"normed{u}", [P, JT, D]) for u in range(2)]
        hT = [sb(f"hT{j}", [P, 2, KC, P]) for j in range(2)]
        rows_now = [sb(f"rows_now{u}", [P, 3], I32) for u in range(2)]
        x_src = [sb(f"x_src{u}", [P, D]) for u in range(2)]
        x_dst = [sb(f"x_dst{u}", [P, D]) for u in range(2)]
        e_in = [sb(f"e_in{u}", [P, D]) for u in range(2)]
        dst_row = [sb(f"dst_row{u}", [P, P + 2]) for u in range(2)]
        edge_normed = [sb(f"edge_normed{u}", [P, 2, D]) for u in range(2)]
        bn = sb("bn", [P, JT + 2, 6])
        stats = [sb(f"stats{u}", [P, JT + 2, 2]) for u in range(2)]
        var_eps = sb("var_eps", [P, JT + 2])
        shift = [sb(f"shift{u}", [P, JT + 2]) for u in range(2)]
        rstd = [sb(f"rstd{u}", [P, JT + 2]) for u in range(2)]
        hT_edge = sb("hT_edge", [P, 2, KC, P])
        eT = sb("eT", [P, KC, P])
        e_sb = sb("e_sb", [P, D])
        q_sb = sb("q_sb", [P, D])
        k_sb = sb("k_sb", [P, D])
        qk = sb("qk", [P, D])
        v_sb = sb("v_sb", [P, D])
        alpha = sb("alpha", [P, H])
        breaks = sb("breaks", [H, P + 1])
        run_max = [sb(f"run_max{u}", [H, P]) for u in range(2)]
        seg_max = sb("seg_max", [H, P])
        rise = sb("rise", [H, 1])
        below = sb("below", [P, H])
        weighted = sb("weighted", [P, H, HD])
        same = [sb(f"same{u}", [P, P]) for u in range(2)]
        carry_to = [sb(f"carry_to{u}", [P, P]) for u in range(2)]
        fade = sb("fade", [P, H])
        sums_sb = sb("sums_sb", [P, H, HD])
        carried = sb("carried", [P, H, HD])
        recip = sb("recip", [P, H])
        attn = sb("attn", [P, D])
        final = sb("final", [P, TILES, D])
        assert PADDED == TILES // 2 * D
        key_row = final[:, 0:TILES // 2, :].rearrange("p t d -> p (t d)")
        half = final[:, TILES // 2:TILES, :].rearrange("p t d -> p (t d)").bitcast(I16)
        number_row = half[:, 0:PADDED]
        mask_row = half[:, PADDED:2 * PADDED].bitcast(BF16)
        SLOTS = 7
        scatter_now = sb("scatter_now", [P, SLOTS], I32)
        assert TILES % SLOTS == 0 and SLOTS <= 2 * JT

        def staged(slot):
            return x_bs[slot // JT][:, slot % JT, :]

        def bank(name):
            return ctx.enter_context(nc.psum_tensor(name, [P, 512], F32))
        ps_hT_edge = bank("ps_hT_edge")
        ps_hT = bank("ps_hT")
        ps_y = [bank(f"ps_y{j}") for j in range(2)]
        ps_sums_bank = bank("ps_sums")
        ps_qs = bank("ps_qs")
        ps_kv = bank("ps_kv")
        ps_e = bank("ps_e")
        ps_sums = ps_sums_bank[:, 0:H * HD]
        ps_alphaT = ps_e[0:H, 0:P]
        ps_seg_max = ps_e[:, P:P + H]
        ps_rise = ps_e[:, P + H:P + 2 * H]
        ps_eT = ps_e[:, 0:D]
        ps_ev = ps_e[:, D:2 * D]
        ps_falls = ps_kv[0:1, 0:TILES]
        ps_tab = ps_qs

        s_weights = sem("weights_loaded")
        s_bias = sem("biases_loaded")
        s_bias_in = sem("bias_row_loaded")
        s_bias_cut = sem("bias_parts_ready")
        s_bias3 = sem("bias3_ready")
        s_bvs = sem("bvs_ready")
        s_const = sem("const_ready")
        s_fill = sem("padding_filled")
        s_raw = sem("raw_indices_loaded")
        s_falls = sem("falls_ready")
        s_falls_T = sem("falls_transposed")
        s_flag = sem("unsorted_ready")
        s_sort_in = sem("sort_rows_loaded")
        s_number_row = sem("number_row_ready")
        s_mask = sem("sort_mask_ready")
        s_count = sem("count_ready")
        s_place = sem("place_ready")
        s_moved = sem("moved")
        s_iota = sem("edge_numbers_ready")
        s_scaled = sem("scaled_dst_ready")
        s_tables = sem("tables_written")
        s_tab_in = sem("tables_loaded")
        s_tab_f = sem("tables_float")
        s_tab_T = sem("tables_transposed")
        s_cols = sem("index_columns_ready")
        s_same_next = sem("same_next_ready")
        s_x = sem2("x_arrived")
        s_row = sem2("dst_row_arrived")
        s_gath = sem2("gathered")
        s_store = sem2("y_stored")
        s_rows_now = sem("rows_now_ready")
        s_bn = sem("bn_ready")
        s_stats = sem("stats_ready")
        s_var = sem("var_eps_ready")
        s_rstd = sem("rstd_ready")
        s_shift = sem("shift_ready")
        s_norm = sem("normed_ready")
        s_edgeT = sem("edge_rows_transposed")
        s_eT = sem("edge_attr_transposed")
        s_nodeT = sem("node_rows_transposed")
        s_hT_edge = sem("hT_edge_ready")
        s_eTs = sem("eT_ready")
        s_hT = sem("hT_ready")
        s_proj = sem("projected")
        s_mm = sem("node_products_done")
        s_xbs = sem("x_bs_ready")
        s_y = sem("y_ready")
        s_e = sem("e_ready")
        s_q = sem("q_ready")
        s_k = sem("k_ready")
        s_qk = sem("qk_ready")
        s_v = sem("v_ready")
        s_part = sem("final_part_ready")
        s_alpha = sem("alpha_ready")
        s_break = sem("breaks_ready")
        s_same = sem("same_ready")
        s_alphaT = sem("alpha_transposed")
        s_run = sem("run_max_ready")
        s_seg = sem("seg_max_ready")
        s_rise = sem("rise_ready")
        s_back = sem("seg_max_back")
        s_below = sem("below_ready")
        s_exp = sem("exp_ready")
        s_fade = sem("fade_ready")
        s_weighted = sem("weighted_ready")
        s_carried = sem("carried_ready")
        s_sums = sem("sums_done")
        s_sums_sb = sem("sums_sb_ready")
        s_recip = sem("recip_ready")
        s_attn = sem("attn_ready")
        s_final = sem("final_ready")
        s_staged = sem("staged_ready")
        s_scat = [sem(f"scattered{k}") for k in range(SLOTS)]

        s_held = sem("waits_held")

        def nodes(n_is_last):
            return (RP, RJ) if n_is_last else (P, JT)

        def wait(eng, s, value):
            if isinstance(value, int) and value <= 0:
                return
            eng.wait_ge(s, value)

        def hold(eng):
            eng.sem_inc(s_held, 1)

        def loop(body, first_peeled=1, last_peeled=1):
            pairs = TILES // 2
            for i in range(first_peeled):
                for u in range(2):
                    body(2 * i + u, i, u)
            yield first_peeled, pairs - last_peeled
            for i in range(pairs - last_peeled, pairs):
                for u in range(2):
                    body(2 * i + u, i, u)

        def run(eng, body, first_peeled=1, last_peeled=1):
            for lo, hi in loop(body, first_peeled, last_peeled):
                with eng.Fori(lo, hi) as i:
                    for u in range(2):
                        body(i * 2 + u, i, u)

        x_groups = x[0:FULL * GROUP, :].rearrange("(g p j) d -> g p j d", p=P, j=JT)
        out_groups = out[0:FULL * GROUP, :].rearrange("(g p j) d -> g p j d", p=P, j=JT)
        x_rest = x[FULL * GROUP:N, :].rearrange("(p j) d -> p j d", j=RJ)
        out_rest = out[FULL * GROUP:N, :].rearrange("(p j) d -> p j d", j=RJ)

        block = ctx.enter_context(nc.Block())

        @block.sync
        def _(sp):
            def load_x(n, u):
                if isinstance(n, int) and n == FULL:
                    sp.dma_start(x_in[u][0:RP, 0:RJ, :], x_rest).then_inc(s_x[u], 16)
                else:
                    sp.dma_start(x_in[u][:, :, :], x_groups[n]).then_inc(s_x[u], 16)

            def load_row(n, u):
                sp.dma_start(dst_row[u][:, :], dst_table[bass.ds(n * P, P + 2)].partition_broadcast(P))\
                    .then_inc(s_row[u], 16)

            def store_y(n, u):
                if isinstance(n, int) and n == FULL:
                    sp.dma_start(out_rest, y_out[u][0:RP, 0:RJ, :]).then_inc(s_store[u], 16)
                else:
                    sp.dma_start(out_groups[n], y_out[u][:, :, :]).then_inc(s_store[u], 16)

            sp.wait_ge(s_fill, 5)
            full = (TILES - 1) * P
            for raw, given, at in ((raw_dst, dst, 0), (raw_next, dst, 1), (raw_src, src, 0)):
                sp.dma_start(raw[0:TILES - 1, :], given[at:at + full].rearrange("(t p) -> t p", p=P))\
                    .then_inc(s_raw, 16)
                sp.dma_start(raw[TILES - 1:TILES, 0:LAST_EDGES - at],
                             given[at + full:E].rearrange("(t p) -> t p", t=1)).then_inc(s_raw, 16)
            load_x(0, 0)
            load_x(1, 1)
            sp.wait_ge(s_raw, 96)
            sp.wait_ge(s_iota, 1)
            sp.wait_ge(s_scaled, 1)
            for table, raw in ((dst_table[1:PADDED + 1], scaled_dst), (src_table[1:PADDED + 1], raw_src),
                               (edge_table[1:PADDED + 1], raw_edge)):
                sp.dma_start(table.rearrange("(t p) -> t p", p=P), raw[:, :]).then_inc(s_tables, 16)
            sp.dma_start(dst_table[0:1].rearrange("(t p) -> t p", t=1), ends[:, 0:1]).then_inc(s_tables, 16)
            sp.dma_start(dst_table[PADDED + 1:PADDED + 2].rearrange("(t p) -> t p", t=1), ends[:, 1:2])\
                .then_inc(s_tables, 16)
            sp.wait_ge(s_tables, 80)
            sp.wait_ge(s_flag, 1)
            with sp.If(sp.value_load(unsorted[0:1, 0:1], min_val=0, max_val=1) > 0):
                sp.dma_start(key_row, dst_table[1:PADDED + 1].partition_broadcast(P)).then_inc(s_sort_in, 16)
                with nc.allow_non_contiguous_dma(reason="columns of the tables, in the sort only"):
                    for col, table in ((key_col, dst_table), (src_col, src_table), (edge_col, edge_table)):
                        sp.dma_start(col[:, :], table[1:PADDED + 1].rearrange("(t p) -> p t", p=P))\
                            .then_inc(s_sort_in, 16)
                sp.wait_ge(s_moved, 48 * TILES)
            for to, table in ((table_f[:, 0, :], dst_table[1:PADDED + 1]),
                              (table_f[:, 1, :], dst_table[2:PADDED + 2]),
                              (table_i[:, 0, :], src_table[1:PADDED + 1]),
                              (table_i[:, 1, :], edge_table[1:PADDED + 1])):
                sp.dma_start(to, table.rearrange("(t p) -> t p", p=P)).then_inc(s_tab_in, 16)
            load_row(0, 0)
            load_row(1, 1)
            for c in range(KC):
                for w, given in ((w_e[:, c, :], We), (w_qs[:, c, 0:D], Wq), (w_qs[:, c, D:2 * D], Ws),
                                 (w_kv[:, c, 0:D], Wk), (w_kv[:, c, D:2 * D], Wv)):
                    sp.dma_start(w, given[c * P:(c + 1) * P, :]).then_inc(s_weights, 16)

            def step(n, i, u):
                last = isinstance(n, int) and n == FULL
                if not (isinstance(n, int) and n + 2 > FULL):
                    sp.wait_ge(s_norm, n * 3 + 3)
                    hold(sp)
                    sp.wait_ge(s_xbs, n + 1)
                    hold(sp)
                    load_x(n + 2, u)
                    sp.wait_ge(s_same, n + 1)
                    hold(sp)
                    load_row(n + 2, u)
                sp.wait_ge(s_y, n * 2 + 2)
                hold(sp)
                store_y(n, u)

            run(sp, step, first_peeled=0, last_peeled=2)
            for u in range(2):
                sp.wait_ge(s_store[u], 16 * (TILES // 2))

        @block.gpsimd
        def _(pool):
            pool.memset(raw_dst[:, :], PAD_DST).then_inc(s_fill, 1)
            pool.memset(raw_next[:, :], PAD_DST).then_inc(s_fill, 1)
            pool.memset(raw_src[:, :], 0).then_inc(s_fill, 1)
            pool.memset(ends[:, 0:1], -APART).then_inc(s_fill, 1)
            pool.memset(ends[:, 1:2], (PAD_DST + 1) * APART).then_inc(s_fill, 1)
            pool.iota(raw_edge[:, :], pattern=[[1, P]], base=0, channel_multiplier=P).then_inc(s_iota, 1)
            pool.memset(ident[:, :], 0.0).then_inc(s_const, 1)
            pool.memset(last_row[:, :], 1.0).then_inc(s_const, 1)
            pool.memset(minus_half[:, :], -0.5).then_inc(s_const, 1)
            pool.memset(sums_sb[:, :, :], 0.0).then_inc(s_const, 1)
            pool.wait_ge(s_const, 4)
            pool.affine_select(out=ident[:, :], in_=ident[:, :], compare_op=ALU.not_equal, fill=1.0,
                               base=0, pattern=[[-1, P]], channel_multiplier=1).then_inc(s_const, 1)
            pool.affine_select(out=last_row[:, :], in_=last_row[:, :], compare_op=ALU.is_ge, fill=0.0,
                               base=-(P - 1), pattern=[[0, 1]], channel_multiplier=1).then_inc(s_const, 1)
            pool.wait_ge(s_bias, 32)
            pool.tensor_tensor(bvs_all[:, :], bvs_all[:, :], bs_all[:, :], ALU.add).then_inc(s_bvs, 1)

            def rstd_of(n, u):
                pool.wait_ge(s_stats, n + 1)
                hold(pool)
                pool.tensor_scalar(var_eps[:, :], stats[u][:, :, 1], EPS, None, ALU.add).then_inc(s_var, 1)
                pool.wait_ge(s_var, n + 1)
                pool.tensor_tensor(rstd[u][:, :], var_eps[:, :], minus_half[:, :], ALU.pow)\
                    .then_inc(s_rstd, 1)

            def gather(n, i, u):
                pool.tensor_copy(rows_now[u][:, :], gather_rows[:, n, :]).then_inc(s_rows_now, 1)
                pool.wait_ge(s_rows_now, n + 1)
                hold(pool)
                for k, (to, table, count) in enumerate(((x_src[u], x, N), (x_dst[u], x, N),
                                                        (e_in[u], edge_attr, E))):
                    pool.indirect_dma_start(
                        out=to[:, :], out_offset=None, in_=table[:, :],
                        in_offset=bass.IndirectOffsetOnAxis(ap=rows_now[u][:, k:k + 1], axis=0),
                        bounds_check=count - 1, oob_is_err=False).then_inc(s_gath[u], 16)

            def x_and_bias(n, i, u):
                p, j = nodes(isinstance(n, int) and n == FULL)
                pool.wait_ge(s_x[u], i * 16 + 16)
                wait(pool, s_y, n * 2 - 2)
                pool.tensor_tensor(x_bs[u][0:p, 0:j, :], x_in[u][0:p, 0:j, :],
                                   bs_all[0:p, :].unsqueeze(1).to_broadcast([p, j, D]), ALU.add)\
                    .then_inc(s_xbs, 1)

            def carry(m, u):
                pool.wait_ge(s_fade, m + 1)
                wait(pool, s_sums_sb, m)
                pool.tensor_tensor(carried[:, :, :], sums_sb[:, :, :],
                                   fade[:, :].unsqueeze(2).to_broadcast([P, H, HD]), ALU.mult)\
                    .then_inc(s_carried, 1)

            def finish(m):
                pool.wait_ge(s_attn, m + 1)
                pool.wait_ge(s_part, m + 1)
                pool.tensor_tensor(final[:, m, :], final[:, m, :], attn[:, :], ALU.add).then_inc(s_final, 1)

            def step(n, i, u):
                first = isinstance(n, int) and n == 0
                last = isinstance(n, int) and n == TILES - 1
                if not (isinstance(n, int) and n < 2):
                    finish(n - 2)
                if not first:
                    carry(n - 1, 1 - u)
                x_and_bias(n, i, u)
                if not last:
                    rstd_of(n + 1, 1 - u)
                if not (isinstance(n, int) and n + 2 > TILES - 1):
                    pool.wait_ge(s_norm, n * 3 + 1)
                    pool.wait_ge(s_eT, n + 1)
                    pool.wait_ge(s_part, n + 1)
                    gather(n + 2, i + 1, u)

            pool.wait_ge(s_flag, 1)
            with pool.If(pool.value_load(unsorted[0:1, 0:1], min_val=0, max_val=1) > 0):
                pool.iota(number_row, pattern=[[1, PADDED]], base=0, channel_multiplier=0,
                          allow_small_or_imprecise_dtypes=True).then_inc(s_number_row, 1)
                pool.wait_ge(s_sort_in, 64)
                with pool.Fori(0, TILES) as t:
                    pool.wait_ge(s_place, t + 1)
                    hold(pool)
                    for table, values in ((dst_table, moved_dst), (src_table, moved_src),
                                          (edge_table, moved_edge)):
                        pool.indirect_dma_start(
                            out=table.rearrange("(a b) -> a b", b=1),
                            out_offset=bass.IndirectOffsetOnAxis(ap=place[:, :], axis=0),
                            in_=values[:, :], in_offset=None,
                            bounds_check=PADDED, oob_is_err=False).then_inc(s_moved, 16)
            pool.wait_ge(s_cols, 3)
            gather(0, 0, 0)
            gather(1, 0, 1)
            rstd_of(0, 0)
            run(pool, step)
            finish(TILES - 2)
            carry(TILES - 1, 1)
            finish(TILES - 1)

            for u in range(2):
                pool.wait_ge(s_store[u], 16 * (TILES // 2))
            with pool.Fori(0, TILES // SLOTS) as i:
                for k in range(SLOTS):
                    pool.wait_ge(s_staged, i * SLOTS + (k + 1))
                    hold(pool)
                    pool.indirect_dma_start(
                        out=out[:, :],
                        out_offset=bass.IndirectOffsetOnAxis(ap=scatter_now[:, k:k + 1], axis=0),
                        in_=staged(k), in_offset=None,
                        bounds_check=N - 1, oob_is_err=False).then_inc(s_scat[k], 16)
            for k in range(SLOTS):
                pool.wait_ge(s_scat[k], 16 * (TILES // SLOTS))

        @block.scalar
        def _(act):
            for b, given in ((bs_all, bs), (bvs_all, bv)):
                act.dma_start(b[:, :], given.partition_broadcast(P)).then_inc(s_bias, 16)
            for k, given in enumerate((bq, bk)):
                act.dma_start(bias_row[:, k * D:(k + 1) * D], given.rearrange("(a b) -> a b", a=1))\
                    .then_inc(s_bias_in, 16)
            act.wait_ge(s_bias_cut, 6)
            for k in range(3):
                act.dma_start(bias3[k:k + 1, :], bias_part[k][:, :]).then_inc(s_bias3, 16)

            def exps(m, u):
                act.wait_ge(s_below, m + 1)
                act.activation(weighted[:, :, C], below[:, :], ACT.Exp, scale=SCALE).then_inc(s_exp, 1)
                act.wait_ge(s_back, m + 1)
                act.activation(fade[:, :], ps_rise, ACT.Exp, scale=-SCALE).then_inc(s_fade, 1)

            def normalise_edges(n, u):
                act.wait_ge(s_shift, n + 1)
                wait(act, s_edgeT, n - 1)
                for k, rows in enumerate((x_src[u], x_dst[u])):
                    done = act.activation(edge_normed[u][:, k, :], rows[:, :], ACT.Relu,
                                          scale=rstd[u][:, k:k + 1], bias=shift[u][:, k:k + 1])
                done.then_inc(s_norm, 1)

            def normalise_nodes(n, u):
                p, tiles = nodes(isinstance(n, int) and n == FULL)
                wait(act, s_nodeT, n * 2 - 2)
                for j in range(JT):
                    if j < tiles:
                        done = act.activation(normed[u][0:p, j, :], x_in[u][0:p, j, :], ACT.Relu,
                                              scale=rstd[u][0:p, 2 + j:3 + j],
                                              bias=shift[u][0:p, 2 + j:3 + j])
                    if j % 2:
                        done.then_inc(s_norm, 1)

            def node_hT(n, j):
                act.wait_ge(s_nodeT, n * 2 + j + 1)
                wait(act, s_mm, n * 2 + j - 1)
                p, tiles = nodes(isinstance(n, int) and n == FULL)
                count = min(2, tiles - 2 * j)
                act.activation(hT[j][:, 0:count, :, 0:p],
                               ps_hT[:, :].rearrange("a (t c p) -> a t c p", t=2, c=KC)[:, 0:count, :, 0:p],
                               ACT.Copy).then_inc(s_hT, 1)

            def keep_sums(m):
                act.wait_ge(s_sums, m + 1)
                wait(act, s_attn, m)
                act.activation(sums_sb[:, :, :], ps_sums.rearrange("p (h c) -> p h c", c=HD),
                               ACT.Copy).then_inc(s_sums_sb, 1)

            def step(n, i, u):
                first = isinstance(n, int) and n == 0
                act.wait_ge(s_edgeT, n + 1)
                wait(act, s_proj, n * 3)
                act.activation(hT_edge[:, :, :, :],
                               ps_hT_edge[:, :].rearrange("a (t c p) -> a t c p", t=2, c=KC),
                               ACT.Copy).then_inc(s_hT_edge, 1)
                if not first:
                    exps(n - 1, 1 - u)
                node_hT(n, 0)
                act.wait_ge(s_proj, n * 3 + 1)
                wait(act, s_qk, n)
                act.activation(q_sb[:, :], ps_qs[:, 0:D], ACT.Copy).then_inc(s_q, 1)
                act.wait_ge(s_eT, n + 1)
                act.activation(eT[:, :, :], ps_eT.rearrange("a (c p) -> a c p", c=KC), ACT.Copy)\
                    .then_inc(s_eTs, 1)
                act.wait_ge(s_proj, n * 3 + 3)
                wait(act, s_v, n)
                act.activation(e_sb[:, :], ps_ev, ACT.Copy).then_inc(s_e, 1)
                node_hT(n, 1)
                last = isinstance(n, int) and n == TILES - 1
                if not last:
                    normalise_edges(n + 1, 1 - u)
                if not first:
                    keep_sums(n - 1)
                if not last:
                    normalise_nodes(n + 1, 1 - u)

            normalise_edges(0, 0)
            normalise_nodes(0, 0)
            run(act, step)
            exps(TILES - 1, 1)
            keep_sums(TILES - 1)


        @block.vector
        def _(dve):
            dve.memset(ones3[:, :], 1.0).then_inc(s_bias_cut, 1)
            dve.wait_ge(s_bias_in, 32)
            for k in range(3):
                if k:
                    dve.wait_ge(s_bias_cut, 2 * k)
                    dve.tensor_tensor(bias_row[:, :], bias_row[:, :], bias_part[k - 1][:, :], ALU.subtract)\
                        .then_inc(s_bias_cut, 1)
                    dve.wait_ge(s_bias_cut, 2 * k + 1)
                dve.tensor_copy(bias_part[k][:, :], bias_row[:, :]).then_inc(s_bias_cut, 1)
            dve.wait_ge(s_raw, 96)
            dve.tensor_scalar(scaled_dst[:, :], raw_dst[:, :], APART, None, ALU.mult).then_inc(s_scaled, 1)
            dve.tensor_tensor(falls[:, :], raw_dst[:, :], raw_next[:, :], ALU.is_gt).then_inc(s_falls, 1)
            dve.wait_ge(s_falls, 1)
            dve.tensor_reduce(out=row_falls[:, :], in_=falls[:, :], op=ALU.max, axis=AX.X).then_inc(s_falls, 1)
            dve.wait_ge(s_falls_T, 1)
            dve.tensor_reduce(out=unsorted[:, :], in_=ps_falls, op=ALU.max, axis=AX.X).then_inc(s_flag, 1)
            dve.wait_ge(s_flag, 1)
            with dve.If(dve.value_load(unsorted[0:1, 0:1], min_val=0, max_val=1) > 0):
                dve.wait_ge(s_sort_in, 64)
                dve.wait_ge(s_number_row, 1)
                with dve.Fori(0, TILES) as t:
                    dve.tensor_copy(moved_src[:, :], src_col[:, bass.ds(t, 1)])
                    dve.tensor_copy(moved_edge[:, :], edge_col[:, bass.ds(t, 1)]).then_inc(s_mask, 1)
                    dve.tensor_copy(moved_dst[:, :], key_col[:, bass.ds(t, 1)]).then_inc(s_mask, 1)
                    dve.wait_ge(s_mask, t * 6 + 2)
                    dve.tensor_copy(count[:, :], moved_edge[:, :]).then_inc(s_mask, 1)
                    dve.tensor_scalar(mask_row, key_row, moved_dst[:, :], None, ALU.is_equal)\
                        .then_inc(s_mask, 1)
                    dve.wait_ge(s_mask, t * 6 + 4)
                    dve.scalar_tensor_tensor(out=mask_row, in0=number_row, scalar=count[:, :],
                                             in1=mask_row, op0=ALU.is_lt, op1=ALU.mult).then_inc(s_mask, 1)
                    dve.wait_ge(s_mask, t * 6 + 5)
                    dve.scalar_tensor_tensor(out=mask_row, in0=key_row, scalar=moved_dst[:, :],
                                             in1=mask_row, op0=ALU.is_lt, op1=ALU.add).then_inc(s_mask, 1)
                    dve.wait_ge(s_mask, t * 6 + 6)
                    dve.tensor_reduce(out=count[:, :], in_=mask_row, op=ALU.add, axis=AX.X)\
                        .then_inc(s_count, 1)
                    dve.wait_ge(s_count, t + 1)
                    dve.tensor_scalar(place[:, :], count[:, :], 1.0, None, ALU.add).then_inc(s_place, 1)
                    dve.wait_ge(s_moved, t * 48 + 48)
            dve.wait_ge(s_tab_in, 64)
            dve.tensor_copy(table_f[:, 2:4, :], table_i[:, :, :]).then_inc(s_tab_f, 1)
            dve.wait_ge(s_tab_T, 1)
            cols = ps_tab[:, 0:4 * TILES].rearrange("p (k t) -> p k t", k=4)
            dve.memset(dst_col[:, 0:1], -APART)
            dve.tensor_copy(dst_col[:, 1:TILES + 1], cols[:, 0, :]).then_inc(s_same_next, 1)
            dve.tensor_copy(dst_next[:, :], cols[:, 1, :]).then_inc(s_same_next, 1)
            dve.tensor_copy(gather_rows[:, :, 0], cols[:, 2, :]).then_inc(s_cols, 1)
            dve.tensor_scalar(gather_rows[:, :, 1], cols[:, 0, :], 1 / APART, float(N - 1), ALU.mult, ALU.min)\
                .then_inc(s_cols, 1)
            dve.tensor_scalar(gather_rows[:, :, 2], cols[:, 3, :], float(E - 1), None, ALU.min)\
                .then_inc(s_cols, 1)
            dve.wait_ge(s_same_next, 2)
            dve.tensor_tensor(same_next[:, :], dst_col[:, 1:TILES + 1], dst_next[:, :], ALU.is_equal)\
                .then_inc(s_same_next, 1)
            dve.wait_ge(s_same_next, 3)
            dve.scalar_tensor_tensor(out=dst_next[:, :], in0=same_next[:, :], scalar=SKIP * APART,
                                     in1=dst_col[:, 1:TILES + 1], op0=ALU.mult, op1=ALU.add)\
                .then_inc(s_same_next, 1)
            dve.wait_ge(s_same_next, 4)
            dve.tensor_scalar(scatter_rows[:, :], dst_next[:, :], 1 / APART, None, ALU.mult)\
                .then_inc(s_cols, 1)

            def statistics(n, i, u):
                p, tiles = nodes(isinstance(n, int) and n == FULL)
                dve.wait_ge(s_gath[u], i * 48 + 48)
                dve.wait_ge(s_x[u], i * 16 + 16)
                dve.bn_stats(bn[:, 0, :], x_src[u][:, :])
                done = dve.bn_stats(bn[:, 1, :], x_dst[u][:, :])
                for j in range(tiles):
                    done = dve.bn_stats(bn[0:p, 2 + j, :], x_in[u][0:p, j, :])
                done.then_inc(s_bn, 1)
                dve.wait_ge(s_bn, n + 1)
                hold(dve)
                for j in range(JT + 2):
                    done = dve.bn_aggr(stats[u][:, j, :], bn[:, j, :])
                done.then_inc(s_stats, 1)

            def shifts(n, u):
                dve.wait_ge(s_rstd, n + 1)
                dve.scalar_tensor_tensor(out=shift[u][:, :], in0=stats[u][:, :, 0], scalar=-1.0,
                                         in1=rstd[u][:, :], op0=ALU.mult, op1=ALU.mult)\
                    .then_inc(s_shift, 1)

            def y_add(n, i, u, j):
                p, tiles = nodes(isinstance(n, int) and n == FULL)
                count = min(2, tiles - 2 * j)
                dve.wait_ge(s_mm, n * 2 + j + 1)
                if j == 0:
                    dve.wait_ge(s_xbs, n + 1)
                    if not (isinstance(i, int) and i == 0):
                        dve.wait_ge(s_store[u], i * 16)
                dve.tensor_tensor(y_out[u][0:p, 2 * j:2 * j + count, :],
                                  ps_y[j][0:p, 0:count * D].rearrange("p (t d) -> p t d", d=D),
                                  x_bs[u][0:p, 2 * j:2 * j + count, :], ALU.add).then_inc(s_y, 1)

            def head_dim(ap):
                return ap.rearrange("p (h c) -> p h c", c=C)

            def scores(n, i, u, more):
                if more:
                    shifts(n + 1, 1 - u)
                dve.wait_ge(s_proj, n * 3 + 2)
                dve.wait_ge(s_e, n + 1)
                dve.tensor_tensor(k_sb[:, :], ps_kv[:, 0:D], e_sb[:, :], ALU.add).then_inc(s_k, 1)
                wait(dve, s_weighted, n)
                dve.tensor_tensor(v_sb[:, :], ps_kv[:, D:2 * D], e_sb[:, :], ALU.add).then_inc(s_v, 1)
                dve.wait_ge(s_k, n + 1)
                dve.tensor_tensor(qk[:, :], q_sb[:, :], k_sb[:, :], ALU.mult).then_inc(s_qk, 1)
                dve.wait_ge(s_qk, n + 1)
                dve.tensor_reduce(out=alpha[:, :], in_=head_dim(qk[:, :]), op=ALU.add, axis=AX.X)\
                    .then_inc(s_alpha, 1)

            def segments(n, i, u):
                dve.wait_ge(s_row[u], i * 16 + 16)
                row = dst_row[u]
                dve.tensor_tensor(breaks[:, :], row[0:H, 0:P + 1], row[0:H, 1:P + 2], ALU.subtract)\
                    .then_inc(s_break, 1)
                dve.tensor_scalar(carry_to[u][96:P, :], row[96:P, 1:P + 1], dst_col[96:P, bass.ds(n, 1)],
                                  last_row[96:P, :], ALU.is_equal, ALU.mult)
                dve.tensor_scalar(same[u][:, :], row[:, 1:P + 1], dst_col[:, bass.ds(n + 1, 1)], None,
                                  ALU.is_equal).then_inc(s_same, 1)

            def maxima(n, i, u):
                first = isinstance(n, int) and n == 0
                dve.wait_ge(s_break, n + 1)
                dve.wait_ge(s_alphaT, n + 1)
                before = 0.0 if first else run_max[1 - u][:, P - 1:P]
                dve.tensor_tensor_scan(run_max[u][:, :], breaks[:, 0:P], ps_alphaT, before,
                                       ALU.add, ALU.max).then_inc(s_run, 1)
                dve.wait_ge(s_run, n + 1)
                dve.tensor_tensor_scan(seg_max[:, ::-1], breaks[:, P:0:-1], run_max[u][:, ::-1], NEG,
                                       ALU.add, ALU.max).then_inc(s_seg, 1)
                dve.wait_ge(s_seg, n + 1)
                dve.tensor_scalar(rise[:, :], seg_max[:, 0:1], before, 0.0, ALU.subtract, ALU.max)\
                    .then_inc(s_rise, 1)

            def weigh(m):
                dve.wait_ge(s_exp, m + 1)
                dve.wait_ge(s_v, m + 1)
                dve.tensor_tensor(weighted[:, :, 0:C], head_dim(v_sb[:, :]),
                                  weighted[:, :, C:HD].to_broadcast([P, H, C]), ALU.mult)\
                    .then_inc(s_weighted, 1)

            def divide(m):
                sums = sums_sb[:, :, :]
                dve.wait_ge(s_sums_sb, m + 1)
                dve.reciprocal(recip[:, :], sums[:, :, C]).then_inc(s_recip, 1)
                dve.wait_ge(s_recip, m + 1)
                wait(dve, s_final, m)
                dve.tensor_tensor(head_dim(attn[:, :]), sums[:, :, 0:C],
                                  recip[:, :].unsqueeze(2).to_broadcast([P, H, C]), ALU.mult)\
                    .then_inc(s_attn, 1)

            def step(n, i, u):
                first = isinstance(n, int) and n == 0
                last = isinstance(n, int) and n == TILES - 1
                back = i if u else i - 1
                ahead = i + 1 if u else i
                if not first:
                    dve.wait_ge(s_back, n)
                    dve.tensor_tensor(below[:, :], alpha[:, :], ps_seg_max, ALU.subtract)\
                        .then_inc(s_below, 1)
                    y_add(n - 1, back, 1 - u, 1)
                if not last:
                    statistics(n + 1, ahead, 1 - u)
                if not first:
                    weigh(n - 1)
                dve.wait_ge(s_gath[u], i * 48 + 48)
                dve.wait_ge(s_q, n + 1)
                dve.tensor_tensor(final[:, n, :], ps_qs[:, D:2 * D], x_dst[u][:, :], ALU.add)\
                    .then_inc(s_part, 1)
                segments(n, i, u)
                scores(n, i, u, not last)
                y_add(n, i, u, 0)
                maxima(n, i, u)
                if not first:
                    divide(n - 1)

            statistics(0, 0, 0)
            shifts(0, 0)
            run(dve, step)
            m = TILES - 1
            dve.wait_ge(s_back, m + 1)
            dve.tensor_tensor(below[:, :], alpha[:, :], ps_seg_max, ALU.subtract).then_inc(s_below, 1)
            y_add(m, TILES // 2 - 1, 1, 1)
            weigh(m)
            divide(m)

            dve.wait_ge(s_bvs, 1)
            dve.wait_ge(s_final, TILES)
            for u in range(2):
                dve.wait_ge(s_store[u], 16 * (TILES // 2))
            def stage(i, k):
                if not isinstance(i, int):
                    dve.wait_ge(s_scat[k], i * 16)
                t = i * SLOTS + k
                dve.tensor_tensor(staged(k), final[:, t, :], bvs_all[:, :], ALU.add)
                dve.tensor_copy(scatter_now[:, k:k + 1], scatter_rows[:, bass.ds(t, 1)]).then_inc(s_staged, 1)

            for k in range(SLOTS):
                stage(0, k)
            with dve.Fori(1, TILES // SLOTS) as i:
                for k in range(SLOTS):
                    stage(i, k)

        @block.tensor
        def _(pe):
            pe.wait_ge(s_const, 6)
            pe.wait_ge(s_falls, 2)
            pe.transpose(ps_falls, row_falls[:, :], ident[0:TILES, 0:TILES]).then_inc(s_falls_T, 1)
            pe.wait_ge(s_tab_f, 1)
            for k in range(4):
                done = pe.transpose(ps_tab[:, k * TILES:(k + 1) * TILES], table_f[:, k, :],
                                    ident[0:TILES, 0:TILES])
            done.then_inc(s_tab_T, 1)
            pe.wait_ge(s_weights, 16 * 5 * KC)
            pe.wait_ge(s_bias3, 48)
            pe.wait_ge(s_cols, 4)

            def chunk(c):
                return slice(c * P, (c + 1) * P)

            def edge_transposes(n, u):
                pe.wait_ge(s_norm, n * 3 + 1)
                wait(pe, s_hT_edge, n)
                for k in range(2):
                    for c in range(KC):
                        at = (k * KC + c) * P
                        done = pe.transpose(ps_hT_edge[:, at:at + P], edge_normed[u][:, k, chunk(c)],
                                            ident[:, :])
                done.then_inc(s_edgeT, 1)

            def attr_transposes(n, i, u):
                pe.wait_ge(s_gath[u], i * 48 + 48)
                wait(pe, s_below, n)
                wait(pe, s_fade, n)
                for c in range(KC):
                    done = pe.transpose(ps_eT[:, c * P:(c + 1) * P], e_in[u][:, chunk(c)], ident[:, :])
                done.then_inc(s_eT, 1)

            def node_transposes(n, i, u, j):
                p, tiles = nodes(isinstance(n, int) and n == FULL)
                pe.wait_ge(s_norm, n * 3 + 2 + j)
                wait(pe, s_hT, n * 2 + j)
                for k in range(min(2, tiles - 2 * j)):
                    for c in range(KC):
                        at = (k * KC + c) * P
                        done = pe.transpose(ps_hT[:, at:at + p], normed[u][0:p, 2 * j + k, chunk(c)],
                                            ident[0:p, 0:p])
                done.then_inc(s_nodeT, 1)

            def node_products(n, i, u, j, between=None):
                p, tiles = nodes(isinstance(n, int) and n == FULL)
                pe.wait_ge(s_hT, n * 2 + j + 1)
                wait(pe, s_y, n * 2 + j - 1)
                for k in range(min(2, tiles - 2 * j)):
                    if k and between:
                        between()
                    for c in range(KC):
                        done = pe.matmul(ps_y[j][0:p, k * D:(k + 1) * D], hT[j][:, k, c, 0:p],
                                         w_qs[:, c, D:2 * D], start=c == 0, stop=c == KC - 1)
                done.then_inc(s_mm, 1)

            def project_dst(n):
                pe.wait_ge(s_hT_edge, n + 1)
                wait(pe, s_part, n)
                for c in range(KC):
                    pe.matmul(ps_qs[:, :], hT_edge[:, 1, c, :], w_qs[:, c, :], start=c == 0, stop=False)
                pe.matmul(ps_qs[:, 0:D], ones3[:, :], bias3[:, 0:D], start=False, stop=True)\
                    .then_inc(s_proj, 1)

            def project_src(n):
                wait(pe, s_v, n)
                for c in range(KC):
                    pe.matmul(ps_kv[:, :], hT_edge[:, 0, c, :], w_kv[:, c, :], start=c == 0, stop=False)
                pe.matmul(ps_kv[:, 0:D], ones3[:, :], bias3[:, D:2 * D], start=False, stop=True)\
                    .then_inc(s_proj, 1)

            def project_attr(n):
                pe.wait_ge(s_eTs, n + 1)
                for c in range(KC):
                    done = pe.matmul(ps_ev, eT[:, c, :], w_e[:, c, :], start=c == 0, stop=c == KC - 1)
                done.then_inc(s_proj, 1)

            def segment_sums(m, u):
                pe.wait_ge(s_weighted, m + 1)
                pe.wait_ge(s_carried, m + 1)
                pe.wait_ge(s_same, m + 1)
                wait(pe, s_sums_sb, m)
                flat = "p h c -> p (h c)"
                pe.matmul(ps_sums, same[u][:, :], weighted[:, :, :].rearrange(flat), start=True, stop=False)
                pe.matmul(ps_sums, carry_to[u][96:P, :], carried[96:P, :, :].rearrange(flat),
                          start=False, stop=True).then_inc(s_sums, 1)

            def step(n, i, u):
                first = isinstance(n, int) and n == 0
                node_transposes(n, i, u, 0)
                project_dst(n)
                attr_transposes(n, i, u)
                project_src(n)
                project_attr(n)
                node_transposes(n, i, u, 1)
                node_products(n, i, u, 0)
                if not first:
                    segment_sums(n - 1, 1 - u)
                pe.wait_ge(s_e, n + 1)
                pe.wait_ge(s_alpha, n + 1)
                pe.transpose(ps_alphaT, alpha[:, :], ident[:, :]).then_inc(s_alphaT, 1)
                last = isinstance(n, int) and n == TILES - 1
                node_products(n, i, u, 1, None if last else lambda: edge_transposes(n + 1, 1 - u))
                pe.wait_ge(s_rise, n + 1)
                hold(pe)
                pe.transpose(ps_seg_max, seg_max[:, :], ident[0:H, 0:H])
                pe.matmul(ps_rise, rise[:, 0:1].to_broadcast([H, P]), ident[0:H, 0:H],
                          start=True, stop=True).then_inc(s_back, 1)

            edge_transposes(0, 0)
            run(pe, step)
            segment_sums(TILES - 1, 1)


_INS = ["x", "src", "dst", "edge_attr_256", "L0_gnn_Wq", "L0_gnn_bq", "L0_gnn_Wk", "L0_gnn_bk",
        "L0_gnn_Wv", "L0_gnn_bv", "L0_gnn_We", "L0_gnn_Ws", "L0_gnn_bs"]


def kernel(**inputs):
    import numpy as _np
    import concourse.bacc as _bacc
    from concourse import mybir as _mybir
    from concourse.bass_utils import run_bass_kernel_spmd as _run

    nc = _bacc.Bacc("TRN2", target_bir_lowering=False, num_devices=1)
    arrays, args = {}, []
    for name in _INS:
        a = _np.ascontiguousarray(inputs[name])
        arrays[f"in_{name}"] = a
        args.append(nc.dram_tensor(f"in_{name}", a.shape, _mybir.dt.from_np(a.dtype), kind="ExternalInput").ap())
    args.append(nc.dram_tensor("out_rows", inputs["x"].shape, _mybir.dt.float32, kind="ExternalOutput").ap())
    build(nc, *args)
    r = _run(nc, [arrays], core_ids=[0])
    return r.results[0]["out_rows"]
```

```python
from contextlib import ExitStack

import concourse.bass as bass
from concourse import mybir

F32 = mybir.dt.float32
I32 = mybir.dt.int32
BF16 = mybir.dt.bfloat16
I16 = mybir.dt.int16
F32R = mybir.dt.float32r
ALU = mybir.AluOpType
ACT = mybir.ActivationFunctionType
AX = mybir.AxisListType

P = 128


def build(nc, x, src, dst, edge_attr, Wq, bq, Wk, bk, Wv, bv, We, Ws, bs, out):
    N, D = x.shape
    E = src.shape[0]
    C = 32
    H = D // C
    KC = D // P
    HD = C + 1
    SCALE = float(C) ** -0.5
    EPS = 1e-5
    JT = 4
    GROUP = JT * P
    TILES = -(-E // P)
    FULL = N // GROUP
    REST = N - FULL * GROUP
    RJ = 3
    RP = REST // RJ
    assert FULL == TILES - 1 and RP * RJ == REST and RP <= P and TILES % 2 == 0
    LAST_EDGES = E - (TILES - 1) * P
    PADDED = TILES * P
    PAD_DST = 1 << 16
    SKIP = 1 << 17
    LAG = 4
    STORED = 2
    SHIFT = LAG + 2
    NEG = -3.0e38
    APART = 2.0 ** 110
    assert N < PAD_DST

    dst_table = nc.dram_tensor("dst_table", (PADDED + 2,), F32, kind="Internal").ap()
    src_table = nc.dram_tensor("src_table", (PADDED + 2,), I32, kind="Internal").ap()
    edge_table = nc.dram_tensor("edge_table", (PADDED + 2,), I32, kind="Internal").ap()

    ctx = ExitStack()
    with ctx:
        def sb(name, shape, dt=F32):
            return ctx.enter_context(nc.sbuf_tensor(name, shape, dt))

        def sem(name):
            return ctx.enter_context(nc.semaphore(name))

        def sem2(name):
            return [sem(f"{name}{u}") for u in range(2)]

        w_e = sb("w_e", [P, KC, D])
        w_qs = [sb(f"w_qs_{part}", [P, KC, 2 * D], F32R) for part in ("high", "low")]
        w_kv = [sb(f"w_kv_{part}", [P, KC, 2 * D], F32R) for part in ("high", "low")]
        ones3 = sb("ones3", [3, P], BF16)
        bias3 = sb("bias3", [3, 3 * D], BF16)
        bs_all = sb("bs_all", [P, D])
        ident = sb("ident", [P, P])
        minus_half = sb("minus_half", [P, JT + 2])
        last_row = sb("last_row", [P, 1])
        raw_dst = sb("raw_dst", [TILES, P], I32)
        raw_src = sb("raw_src", [TILES, P], I32)
        raw_edge = sb("raw_edge", [TILES, P], I32)
        raw_next = sb("raw_next", [TILES, P], I32)
        falls = sb("falls", [TILES, P])
        row_falls = sb("row_falls", [TILES, 1])
        unsorted = sb("unsorted", [1, 1], I32)
        key_col = sb("key_col", [P, TILES])
        src_col = sb("src_col", [P, TILES], I32)
        edge_col = sb("edge_col", [P, TILES], I32)
        count = sb("count", [P, 1])
        place = sb("place", [P, 1], I32)
        moved_dst = sb("moved_dst", [P, 1])
        moved_src = sb("moved_src", [P, 1], I32)
        moved_edge = sb("moved_edge", [P, 1], I32)
        ends = sb("ends", [1, 2])
        dst_col = sb("dst_col", [P, TILES + 1])
        same_next = sb("same_next", [P, TILES])
        dst_next = sb("dst_next", [P, TILES])
        tile_rows = sb("tile_rows", [P, TILES + SHIFT, 4], I32)
        late = sb("late", [P, 1], I32)
        scatter_rows = sb("scatter_rows", [P, TILES], I32)
        x_in = [sb(f"x_in{u}", [P, JT, D]) for u in range(2)]
        x_bs = [sb(f"x_bs{u}", [P, JT, D]) for u in range(2)]
        y_out = [sb(f"y_out{u}", [P, JT, D]) for u in range(2)]
        normed = [sb(f"normed{u}", [P, JT, D]) for u in range(2)]
        hT = [sb(f"hT_high{j}", [P, 2, KC, P], F32R) for j in range(2)]
        hT_low = [sb(f"hT_low{j}", [P, 2, KC, P], F32R) for j in range(2)]
        rows_now = [sb(f"rows_now{u}", [P, 4], I32) for u in range(2)]
        rows_out = [sb(f"rows_out{u}", [P, D]) for u in range(2)]
        x_src = [sb(f"x_src{u}", [P, D]) for u in range(2)]
        x_dst = [sb(f"x_dst{u}", [P, D]) for u in range(2)]
        e_in = [sb(f"e_in{u}", [P, D]) for u in range(2)]
        dst_row = [sb(f"dst_row{u}", [P, P + 2]) for u in range(2)]
        edge_normed = [sb(f"edge_normed{u}", [P, 2, D]) for u in range(2)]
        bn = sb("bn", [P, JT, 6])
        row_sum = sb("row_sum", [P, 2])
        row_square = sb("row_square", [P, 2])
        stats = [sb(f"stats{u}", [P, JT + 2, 2]) for u in range(2)]
        var_eps = sb("var_eps", [P, JT + 2])
        shift = [sb(f"shift{u}", [P, JT + 2]) for u in range(2)]
        rstd = [sb(f"rstd{u}", [P, JT + 2]) for u in range(2)]
        hT_edge = [sb(f"hT_edge_{part}", [P, 2, KC, P], F32R) for part in ("high", "low")]
        eT = sb("eT", [P, KC, P])
        e_sb = sb("e_sb", [P, D])
        q_sb = sb("q_sb", [P, D])
        k_sb = sb("k_sb", [P, D])
        qk = sb("qk", [P, D])
        v_sb = [sb(f"v_sb{u}", [P, D]) for u in range(2)]
        alpha = [sb(f"alpha{u}", [P, H]) for u in range(2)]
        breaks = [sb(f"breaks{u}", [H, P + 1]) for u in range(2)]
        run_max = [sb(f"run_max{u}", [H, P]) for u in range(2)]
        seg_max = sb("seg_max", [H, P])
        rise = sb("rise", [H, 1])
        below = sb("below", [P, H])
        weighted = sb("weighted", [P, H, HD])
        same = [sb(f"same{u}", [P, P]) for u in range(2)]
        carry_to = [sb(f"carry_to{u}", [P, P]) for u in range(2)]
        fade = sb("fade", [P, H])
        sums_sb = sb("sums_sb", [P, H, HD])
        carried = sb("carried", [P, H, HD])
        recip = sb("recip", [P, H])
        attn = sb("attn", [P, D])
        final = sb("final", [P, TILES, D])
        assert PADDED == TILES // 2 * D
        key_row = final[:, 0:TILES // 2, :].rearrange("p t d -> p (t d)")
        half = final[:, TILES // 2:TILES, :].rearrange("p t d -> p (t d)").bitcast(I16)
        number_row = half[:, 0:PADDED]
        mask_row = half[:, PADDED:2 * PADDED].bitcast(BF16)
        SLOTS = 7
        scatter_now = sb("scatter_now", [P, SLOTS], I32)
        assert TILES % SLOTS == 0 and SLOTS <= 2 * JT

        def staged(slot):
            return x_bs[slot // JT][:, slot % JT, :]

        def bank(name):
            return ctx.enter_context(nc.psum_tensor(name, [P, 512], F32))
        ps_hT_edge = bank("ps_hT_edge")
        ps_hT = bank("ps_hT")
        ps_y = [bank(f"ps_y{j}") for j in range(2)]
        ps_sums_bank = bank("ps_sums")
        ps_qs = bank("ps_qs")
        ps_kv = bank("ps_kv")
        ps_e = bank("ps_e")
        ps_sums = ps_sums_bank[:, 0:H * HD]
        ps_alphaT = ps_e[0:H, 0:P]
        ps_seg_max = ps_e[:, P:P + H]
        ps_rise = ps_e[:, P + H:P + 2 * H]
        ps_eT = ps_e[:, 0:D]
        ps_ev = ps_e[:, D:2 * D]
        ps_falls = ps_kv[0:1, 0:TILES]
        ps_tab = ps_qs

        given_qs = y_out[0][:, :, :].rearrange("p j d -> p (j d)").rearrange("p (c n) -> p c n", c=KC)
        given_kv = y_out[1][:, :, :].rearrange("p j d -> p (j d)").rearrange("p (c n) -> p c n", c=KC)
        SPLITS = ((w_qs, given_qs), (w_kv, given_kv))

        spare_row = x_bs[1][0:1, :, :].rearrange("p j d -> p (j d)")
        bias_row = spare_row[:, 0:3 * D]
        bs_row = spare_row[:, 3 * D:4 * D]
        bias_part = [x_bs[0][0:1, :, :].rearrange("p j d -> p (j d)").bitcast(BF16)[:, 0:3 * D],
                     x_bs[0][0:1, :, :].rearrange("p j d -> p (j d)").bitcast(BF16)[:, 3 * D:6 * D],
                     edge_normed[0][0:1, :, :].rearrange("p k d -> p (k d)").bitcast(BF16)[:, 0:3 * D]]
        limit = carried[:, :, :].rearrange("p h c -> p (h c)")[:, 0:TILES]
        over = final[:, TILES - 1, 0:TILES]
        loop_rows = final[:, TILES - 1, TILES:2 * TILES]
        table_f = edge_normed[1][0:TILES, :, :].rearrange("t k (a p) -> t (k a) p", p=P)

        s_weights = sem("weights_loaded")
        s_bias = sem("biases_loaded")
        s_w_high = sem("weights_high_ready")
        s_w_low = sem("weights_low_ready")
        s_hT_low = sem("hT_edge_low_ready")
        s_bias_in = sem("bias_row_loaded")
        s_bias_cut = sem("bias_parts_ready")
        s_bias3 = sem("bias3_ready")
        s_const = sem("const_ready")
        s_fill = sem("padding_filled")
        s_raw = sem("raw_indices_loaded")
        s_falls = sem("falls_ready")
        s_falls_T = sem("falls_transposed")
        s_flag = sem("unsorted_ready")
        s_sort_in = sem("sort_rows_loaded")
        s_number_row = sem("number_row_ready")
        s_mask = sem("sort_mask_ready")
        s_count = sem("count_ready")
        s_place = sem("place_ready")
        s_moved = sem("moved")
        s_iota = sem("edge_numbers_ready")
        s_scaled = sem("scaled_dst_ready")
        s_tables = sem("tables_written")
        s_tab_in = sem("tables_loaded")
        s_tab_f = sem("tables_float")
        s_tab_T = sem("tables_transposed")
        s_cols = sem("index_columns_ready")
        s_same_next = sem("same_next_ready")
        s_x = sem2("x_arrived")
        s_row = sem2("dst_row_arrived")
        s_gath = sem2("gathered")
        s_store = sem2("y_stored")
        s_rows_now = sem2("rows_now_loaded")
        s_bn = sem("bn_ready")
        s_stats = sem("stats_ready")
        s_sum = sem("row_sum_ready")
        s_mean = sem("row_mean_ready")
        s_square = sem("row_square_ready")
        s_node_stats = sem("node_stats_ready")
        s_var = sem("var_eps_ready")
        s_rstd = sem("rstd_ready")
        s_shift = sem("shift_ready")
        s_norm = sem("normed_ready")
        s_edgeT = sem("edge_rows_transposed")
        s_eT = sem("edge_attr_transposed")
        s_nodeT = sem("node_rows_transposed")
        s_hT_edge = sem("hT_edge_ready")
        s_eTs = sem("eT_ready")
        s_hT = sem("hT_ready")
        s_hT_low_nodes = sem("hT_low_ready")
        s_proj = sem("projected")
        s_mm = sem("node_products_done")
        s_xbs = sem("x_bs_ready")
        s_y = sem("y_ready")
        s_e = sem("e_ready")
        s_q = sem("q_ready")
        s_k = sem("k_ready")
        s_qk = sem("qk_ready")
        s_v = sem("v_ready")
        s_part = sem("final_part_ready")
        s_alpha = sem("alpha_ready")
        s_break = sem("breaks_ready")
        s_same = sem("same_ready")
        s_alphaT = sem("alpha_transposed")
        s_run = sem("run_max_ready")
        s_seg = sem("seg_max_ready")
        s_rise = sem("rise_ready")
        s_back = sem("seg_max_back")
        s_below = sem("below_ready")
        s_exp = sem("exp_ready")
        s_fade = sem("fade_ready")
        s_weighted = sem("weighted_ready")
        s_carried = sem("carried_ready")
        s_sums = sem("sums_done")
        s_sums_sb = sem("sums_sb_ready")
        s_recip = sem("recip_ready")
        s_attn = sem("attn_ready")
        s_final = sem("final_ready")
        s_staged = sem("staged_ready")
        s_late = sem("late_ready")
        s_over = sem("over_ready")
        s_limit = sem("limit_ready")
        s_out = sem2("rows_out_loaded")
        s_scattered = sem2("rows_out_scattered")
        s_last = sem("last_rows_scattered")
        s_scat = [sem(f"scattered_again{k}") for k in range(SLOTS)]

        s_held = sem("waits_held")

        def nodes(n_is_last):
            return (RP, RJ) if n_is_last else (P, JT)

        def wait(eng, s, value):
            if isinstance(value, int) and value <= 0:
                return
            eng.wait_ge(s, value)

        def hold(eng):
            eng.sem_inc(s_held, 1)

        def loop(body, first_peeled=1, last_peeled=1):
            pairs = TILES // 2
            for i in range(first_peeled):
                for u in range(2):
                    body(2 * i + u, i, u)
            yield first_peeled, pairs - last_peeled
            for i in range(pairs - last_peeled, pairs):
                for u in range(2):
                    body(2 * i + u, i, u)

        def run(eng, body, first_peeled=1, last_peeled=1):
            for lo, hi in loop(body, first_peeled, last_peeled):
                with eng.Fori(lo, hi) as i:
                    for u in range(2):
                        body(i * 2 + u, i, u)

        x_groups = x[0:FULL * GROUP, :].rearrange("(g p j) d -> g p j d", p=P, j=JT)
        out_groups = out[0:FULL * GROUP, :].rearrange("(g p j) d -> g p j d", p=P, j=JT)
        x_rest = x[FULL * GROUP:N, :].rearrange("(p j) d -> p j d", j=RJ)
        out_rest = out[FULL * GROUP:N, :].rearrange("(p j) d -> p j d", j=RJ)

        block = ctx.enter_context(nc.Block())

        @block.sync
        def _(sp):
            def load_x(n, u):
                if isinstance(n, int) and n == FULL:
                    sp.dma_start(x_in[u][0:RP, 0:RJ, :], x_rest).then_inc(s_x[u], 16)
                else:
                    sp.dma_start(x_in[u][:, :, :], x_groups[n]).then_inc(s_x[u], 16)

            def load_row(n, u):
                sp.dma_start(dst_row[u][:, :], dst_table[bass.ds(n * P, P + 2)].partition_broadcast(P))\
                    .then_inc(s_row[u], 16)

            def store_y(n, u):
                if isinstance(n, int) and n == FULL:
                    sp.dma_start(out_rest, y_out[u][0:RP, 0:RJ, :]).then_inc(s_store[u], 16)
                else:
                    sp.dma_start(out_groups[n], y_out[u][:, :, :]).then_inc(s_store[u], 16)

            sp.wait_ge(s_fill, 5)
            full = (TILES - 1) * P
            for raw, given, at in ((raw_dst, dst, 0), (raw_next, dst, 1), (raw_src, src, 0)):
                sp.dma_start(raw[0:TILES - 1, :], given[at:at + full].rearrange("(t p) -> t p", p=P))\
                    .then_inc(s_raw, 16)
                sp.dma_start(raw[TILES - 1:TILES, 0:LAST_EDGES - at],
                             given[at + full:E].rearrange("(t p) -> t p", t=1)).then_inc(s_raw, 16)
            load_x(0, 0)
            load_x(1, 1)
            for c in range(KC):
                for w, given in ((given_qs[:, c, 0:D], Wq), (given_qs[:, c, D:2 * D], Ws),
                                 (given_kv[:, c, 0:D], Wk), (given_kv[:, c, D:2 * D], Wv),
                                 (w_e[:, c, :], We)):
                    sp.dma_start(w, given[c * P:(c + 1) * P, :]).then_inc(s_weights, 16)
            sp.wait_ge(s_raw, 96)
            sp.wait_ge(s_iota, 1)
            sp.wait_ge(s_scaled, 1)
            for table, raw in ((dst_table[1:PADDED + 1], table_f[:, 0, :]),
                               (src_table[1:PADDED + 1], raw_src[:, :]),
                               (edge_table[1:PADDED + 1], raw_edge[:, :])):
                sp.dma_start(table.rearrange("(t p) -> t p", p=P), raw).then_inc(s_tables, 16)
            sp.dma_start(dst_table[0:1].rearrange("(t p) -> t p", t=1), ends[:, 0:1]).then_inc(s_tables, 16)
            sp.dma_start(dst_table[PADDED + 1:PADDED + 2].rearrange("(t p) -> t p", t=1), ends[:, 1:2])\
                .then_inc(s_tables, 16)
            sp.wait_ge(s_tables, 80)
            sp.wait_ge(s_flag, 1)
            with sp.If(sp.value_load(unsorted[0:1, 0:1], min_val=0, max_val=1) > 0):
                sp.dma_start(key_row, dst_table[1:PADDED + 1].partition_broadcast(P)).then_inc(s_sort_in, 16)
                with nc.allow_non_contiguous_dma(reason="columns of the tables, in the sort only"):
                    for col, table in ((key_col, dst_table), (src_col, src_table), (edge_col, edge_table)):
                        sp.dma_start(col[:, :], table[1:PADDED + 1].rearrange("(t p) -> p t", p=P))\
                            .then_inc(s_sort_in, 16)
                sp.wait_ge(s_moved, 48 * TILES)
                for to, table in ((table_f[:, 0, :], dst_table[1:PADDED + 1]),
                                  (table_f[:, 1, :], dst_table[2:PADDED + 2]),
                                  (raw_src[:, :], src_table[1:PADDED + 1]),
                                  (raw_edge[:, :], edge_table[1:PADDED + 1])):
                    sp.dma_start(to, table.rearrange("(t p) -> t p", p=P)).then_inc(s_tab_in, 16)
            load_row(0, 0)
            load_row(1, 1)

            def load_final(n, i, u):
                sp.wait_ge(s_final, n - LAG + 1)
                hold(sp)
                if not isinstance(i, int) or i > LAG // 2:
                    sp.wait_ge(s_scattered[u], (i - LAG // 2) * 16)
                    hold(sp)
                sp.dma_start(rows_out[u][:, :], final[:, n - LAG, :]).then_inc(s_out[u], 16)

            def load_indices(n, i, u):
                sp.wait_ge(s_gath[u], i * 48)
                hold(sp)
                if not isinstance(i, int) or i > LAG // 2 + 1:
                    sp.wait_ge(s_scattered[u], (i - 1 - LAG // 2) * 16)
                    hold(sp)
                sp.dma_start(rows_now[u][:, :], tile_rows[:, n, :]).then_inc(s_rows_now[u], 16)

            def step(n, i, u):
                more = not (isinstance(n, int) and n + 2 > FULL)
                if more:
                    sp.wait_ge(s_norm, n * 3 + 3)
                    hold(sp)
                    sp.wait_ge(s_xbs, n + 1)
                    hold(sp)
                    load_x(n + 2, u)
                sp.wait_ge(s_y, n * 2 + 2)
                hold(sp)
                store_y(n, u)
                if not (isinstance(n, int) and n + 3 > FULL):
                    load_indices(n + 3, i + 1 + u, 1 - u)
                if not isinstance(n, int) or LAG <= n + 1 < TILES - 2:
                    load_final(n + 1, i + u, 1 - u)
                if more:
                    sp.wait_ge(s_same, n + 1)
                    hold(sp)
                    sp.wait_ge(s_break, n + 1)
                    hold(sp)
                    load_row(n + 2, u)

            sp.wait_ge(s_cols, 4)
            load_indices(2, 1, 0)
            run(sp, step, first_peeled=3, last_peeled=2)
            for u in range(2):
                sp.wait_ge(s_store[u], 16 * (TILES // 2))

        @block.gpsimd
        def _(pool):
            pool.memset(raw_dst[:, :], PAD_DST).then_inc(s_fill, 1)
            pool.memset(raw_next[:, :], PAD_DST).then_inc(s_fill, 1)
            pool.memset(raw_src[:, :], 0).then_inc(s_fill, 1)
            pool.memset(ends[:, 0:1], -APART).then_inc(s_fill, 1)
            pool.memset(ends[:, 1:2], (PAD_DST + 1) * APART).then_inc(s_fill, 1)
            pool.iota(limit[:, :], pattern=[[GROUP, TILES]], base=GROUP * (LAG - STORED + 1),
                      channel_multiplier=0, allow_small_or_imprecise_dtypes=True).then_inc(s_limit, 1)
            pool.wait_ge(s_limit, 1)
            pool.memset(limit[:, TILES - LAG:TILES], 2 * PAD_DST).then_inc(s_limit, 1)
            pool.memset(tile_rows[:, 0:SHIFT, :], 0).then_inc(s_limit, 1)
            pool.iota(raw_edge[:, :], pattern=[[1, P]], base=0, channel_multiplier=P).then_inc(s_iota, 1)
            pool.memset(ident[:, :], 0.0).then_inc(s_const, 1)
            pool.memset(last_row[:, :], 1.0).then_inc(s_const, 1)
            pool.memset(minus_half[:, :], -0.5).then_inc(s_const, 1)
            pool.memset(sums_sb[:, :, :], 0.0).then_inc(s_const, 1)
            pool.wait_ge(s_const, 4)
            pool.affine_select(out=ident[:, :], in_=ident[:, :], compare_op=ALU.not_equal, fill=1.0,
                               base=0, pattern=[[-1, P]], channel_multiplier=1).then_inc(s_const, 1)
            pool.affine_select(out=last_row[:, :], in_=last_row[:, :], compare_op=ALU.is_ge, fill=0.0,
                               base=-(P - 1), pattern=[[0, 1]], channel_multiplier=1).then_inc(s_const, 1)
            pool.wait_ge(s_bias, 16)

            def rstd_of(n, u):
                pool.wait_ge(s_stats, n + 1)
                pool.wait_ge(s_node_stats, n + 1)
                hold(pool)
                pool.tensor_scalar(var_eps[:, :], stats[u][:, :, 1], EPS, None, ALU.add).then_inc(s_var, 1)
                pool.wait_ge(s_var, n + 1)
                pool.tensor_tensor(rstd[u][:, :], var_eps[:, :], minus_half[:, :], ALU.pow)\
                    .then_inc(s_rstd, 1)

            def gather(n, i, u):
                if isinstance(n, int) and n < 2:
                    rows = tile_rows[:, n, :]
                else:
                    pool.wait_ge(s_rows_now[u], i * 16)
                    hold(pool)
                    rows = rows_now[u][:, :]
                for k, (to, table, count) in enumerate(((x_src[u], x, N), (x_dst[u], x, N),
                                                        (e_in[u], edge_attr, E))):
                    pool.indirect_dma_start(
                        out=to[:, :], out_offset=None, in_=table[:, :],
                        in_offset=bass.IndirectOffsetOnAxis(ap=rows[:, k:k + 1], axis=0),
                        bounds_check=count - 1, oob_is_err=False).then_inc(s_gath[u], 16)

            def scatter_final(m, done):
                pool.wait_ge(s_final, m + 1)
                pool.indirect_dma_start(
                    out=out[:, :],
                    out_offset=bass.IndirectOffsetOnAxis(ap=tile_rows[:, m + SHIFT, 3:4], axis=0),
                    in_=final[:, m, :], in_offset=None,
                    bounds_check=N - 1, oob_is_err=False).then_inc(done, 16)

            def scatter(n, i, u):
                pool.wait_ge(s_store[u], i * 16)
                pool.wait_ge(s_store[1 - u], (i - 1 + u) * 16)
                if isinstance(n, int) and n >= TILES - 2:
                    scatter_final(n - LAG, s_scattered[u])
                    return
                pool.wait_ge(s_out[u], (i - LAG // 2 + 1) * 16)
                hold(pool)
                pool.indirect_dma_start(
                    out=out[:, :],
                    out_offset=bass.IndirectOffsetOnAxis(ap=rows_now[u][:, 3:4], axis=0),
                    in_=rows_out[u][:, :], in_offset=None,
                    bounds_check=N - 1, oob_is_err=False).then_inc(s_scattered[u], 16)

            def x_and_bias(n, i, u):
                p, j = nodes(isinstance(n, int) and n == FULL)
                pool.wait_ge(s_x[u], i * 16 + 16)
                wait(pool, s_y, n * 2 - 2)
                pool.tensor_tensor(x_bs[u][0:p, 0:j, :], x_in[u][0:p, 0:j, :],
                                   bs_all[0:p, :].unsqueeze(1).to_broadcast([p, j, D]), ALU.add)\
                    .then_inc(s_xbs, 1)

            def breaks_of(n, i, u):
                pool.wait_ge(s_row[u], i * 16 + 16)
                wait(pool, s_seg, n - 1)
                pool.tensor_tensor(breaks[u][:, :], dst_row[u][0:H, 0:P + 1], dst_row[u][0:H, 1:P + 2],
                                   ALU.subtract).then_inc(s_break, 1)

            def carry(m):
                pool.wait_ge(s_fade, m + 1)
                wait(pool, s_sums_sb, m)
                pool.tensor_tensor(carried[:, :, :], sums_sb[:, :, :],
                                   fade[:, :].unsqueeze(2).to_broadcast([P, H, HD]), ALU.mult)\
                    .then_inc(s_carried, 1)

            def step(n, i, u):
                last = isinstance(n, int) and n == TILES - 1
                x_and_bias(n, i, u)
                if not (isinstance(n, int) and n < 2):
                    carry(n - 2)
                more = not (isinstance(n, int) and n + 2 > TILES - 1)
                breaks_of(n, i, u)
                if not last:
                    rstd_of(n + 1, 1 - u)
                if more:
                    pool.wait_ge(s_norm, n * 3 + 1)
                    pool.wait_ge(s_eT, n + 1)
                    pool.wait_ge(s_part, n + 1)
                    gather(n + 2, i + 1, u)
                if not (isinstance(n, int) and n < LAG):
                    scatter(n, i, u)

            pool.wait_ge(s_flag, 1)
            with pool.If(pool.value_load(unsorted[0:1, 0:1], min_val=0, max_val=1) > 0):
                pool.iota(number_row, pattern=[[1, PADDED]], base=0, channel_multiplier=0,
                          allow_small_or_imprecise_dtypes=True).then_inc(s_number_row, 1)
                pool.wait_ge(s_sort_in, 64)
                with pool.Fori(0, TILES) as t:
                    pool.wait_ge(s_place, t + 1)
                    hold(pool)
                    for table, values in ((dst_table, moved_dst), (src_table, moved_src),
                                          (edge_table, moved_edge)):
                        pool.indirect_dma_start(
                            out=table.rearrange("(a b) -> a b", b=1),
                            out_offset=bass.IndirectOffsetOnAxis(ap=place[:, :], axis=0),
                            in_=values[:, :], in_offset=None,
                            bounds_check=PADDED, oob_is_err=False).then_inc(s_moved, 16)
            pool.wait_ge(s_cols, 3)
            for u in range(2):
                gather(u, 0, u)
            rstd_of(0, 0)
            pool.wait_ge(s_cols, 4)
            pool.wait_ge(s_bias3, 48)
            run(pool, step, first_peeled=3)
            carry(TILES - 2)
            carry(TILES - 1)

            for u in range(2):
                pool.wait_ge(s_store[u], 16 * (TILES // 2))
            for m in range(TILES - LAG, TILES):
                scatter_final(m, s_last)
            for u in range(2):
                pool.wait_ge(s_scattered[u], 16 * ((TILES - LAG) // 2))
            pool.wait_ge(s_last, 16 * LAG)
            pool.wait_ge(s_late, 1)
            with pool.If(pool.value_load(late[P - 1:P, 0:1], min_val=0, max_val=1) > 0):
                with pool.Fori(0, TILES // SLOTS) as i:
                    for k in range(SLOTS):
                        pool.wait_ge(s_staged, i * SLOTS + (k + 1))
                        hold(pool)
                        pool.indirect_dma_start(
                            out=out[:, :],
                            out_offset=bass.IndirectOffsetOnAxis(ap=scatter_now[:, k:k + 1], axis=0),
                            in_=staged(k), in_offset=None,
                            bounds_check=N - 1, oob_is_err=False).then_inc(s_scat[k], 16)
                for k in range(SLOTS):
                    pool.wait_ge(s_scat[k], 16 * (TILES // SLOTS))

        @block.scalar
        def _(act):
            act.dma_start(bs_all[:, :], bs.partition_broadcast(P)).then_inc(s_bias, 16)
            for k, given in enumerate((bq, bv, bk)):
                act.dma_start(bias_row[:, k * D:(k + 1) * D], given.rearrange("(a b) -> a b", a=1))\
                    .then_inc(s_bias_in, 16)
            act.dma_start(bs_row[:, :], bs.rearrange("(a b) -> a b", a=1)).then_inc(s_bias_in, 16)

            def exps(m):
                act.wait_ge(s_below, m + 1)
                act.activation(weighted[:, :, C], below[:, :], ACT.Exp, scale=SCALE).then_inc(s_exp, 1)
                act.wait_ge(s_back, m + 1)
                act.activation(fade[:, :], ps_rise, ACT.Exp, scale=-SCALE).then_inc(s_fade, 1)

            def row_sums(n, i, u):
                p, tiles = nodes(isinstance(n, int) and n == FULL)
                act.wait_ge(s_x[u], i * 16 + 16)
                wait(act, s_nodeT, n * 2 - 2)
                for j in range(2, tiles):
                    done = act.activation(normed[u][0:p, j, :], x_in[u][0:p, j, :], ACT.Copy,
                                          accum_out=row_sum[0:p, j - 2:j - 1])
                done.then_inc(s_sum, 1)

            def statistics(n, i, u):
                p, tiles = nodes(isinstance(n, int) and n == FULL)
                act.wait_ge(s_sum, n + 1)
                act.activation(stats[u][:, 4:6, 0], row_sum[:, :], ACT.Copy, scale=1 / D)\
                    .then_inc(s_mean, 1)
                act.wait_ge(s_mean, n + 1)
                for j in range(2, tiles):
                    done = act.activation(normed[u][0:p, j, :], x_in[u][0:p, j, :], ACT.Square, scale=-1.0,
                                          bias=stats[u][0:p, 2 + j, 0:1],
                                          accum_out=row_square[0:p, j - 2:j - 1])
                done.then_inc(s_square, 1)
                act.wait_ge(s_square, n + 1)
                act.activation(stats[u][:, 4:6, 1], row_square[:, :], ACT.Copy, scale=1 / D)\
                    .then_inc(s_node_stats, 1)

            def normalise_edges(n, u):
                act.wait_ge(s_shift, n + 1)
                wait(act, s_edgeT, n - 1)
                for k, rows in enumerate((x_src[u], x_dst[u])):
                    done = act.activation(edge_normed[u][:, k, :], rows[:, :], ACT.Relu,
                                          scale=rstd[u][:, k:k + 1], bias=shift[u][:, k:k + 1])
                done.then_inc(s_norm, 1)

            def normalise_nodes(n, u, pair):
                p, tiles = nodes(isinstance(n, int) and n == FULL)
                wait(act, s_nodeT, n * 2 - 2)
                for j in (2 * pair, 2 * pair + 1):
                    if j < tiles:
                        done = act.activation(normed[u][0:p, j, :], x_in[u][0:p, j, :], ACT.Relu,
                                              scale=rstd[u][0:p, 2 + j:3 + j],
                                              bias=shift[u][0:p, 2 + j:3 + j])
                    if j % 2:
                        done.then_inc(s_norm, 1)

            def node_hT(n, j):
                act.wait_ge(s_nodeT, n * 2 + j + 1)
                wait(act, s_mm, n * 2 + j - 1)
                p, tiles = nodes(isinstance(n, int) and n == FULL)
                count = min(2, tiles - 2 * j)
                act.activation(hT[j][:, 0:count, :, 0:p],
                               ps_hT[:, :].rearrange("a (t c p) -> a t c p", t=2, c=KC)[:, 0:count, :, 0:p],
                               ACT.Copy).then_inc(s_hT, 1)

            def keep_sums(m):
                act.wait_ge(s_sums, m + 1)
                wait(act, s_attn, m)
                act.activation(sums_sb[:, :, :], ps_sums.rearrange("p (h c) -> p h c", c=HD),
                               ACT.Copy).then_inc(s_sums_sb, 1)

            def step(n, i, u):
                first = isinstance(n, int) and n < 2
                act.wait_ge(s_edgeT, n + 1)
                wait(act, s_proj, n * 3)
                act.activation(hT_edge[0][:, :, :, :],
                               ps_hT_edge[:, :].rearrange("a (t c p) -> a t c p", t=2, c=KC),
                               ACT.Copy).then_inc(s_hT_edge, 1)
                normalise_nodes(n, u, 1)
                if not first:
                    exps(n - 2)
                node_hT(n, 0)
                if not (isinstance(n, int) and n == TILES - 1):
                    row_sums(n + 1, i + u, 1 - u)
                act.wait_ge(s_proj, n * 3 + 1)
                wait(act, s_qk, n)
                act.activation(q_sb[:, :], ps_qs[:, 0:D], ACT.Copy).then_inc(s_q, 1)
                act.wait_ge(s_eT, n + 1)
                act.activation(eT[:, :, :], ps_eT.rearrange("a (c p) -> a c p", c=KC), ACT.Copy)\
                    .then_inc(s_eTs, 1)
                if not (isinstance(n, int) and n == TILES - 1):
                    statistics(n + 1, i + u, 1 - u)
                act.wait_ge(s_proj, n * 3 + 3)
                wait(act, s_v, n)
                act.activation(e_sb[:, :], ps_ev, ACT.Copy).then_inc(s_e, 1)
                node_hT(n, 1)
                last = isinstance(n, int) and n == TILES - 1
                if not first:
                    keep_sums(n - 2)
                if not last:
                    normalise_edges(n + 1, 1 - u)
                    normalise_nodes(n + 1, 1 - u, 0)

            act.wait_ge(s_weights, 16 * 5 * KC)
            for (high, low), given in SPLITS:
                act.activation(high[:, :, :], given, ACT.Copy).then_inc(s_w_high, 1)
            row_sums(0, 0, 0)
            statistics(0, 0, 0)
            act.wait_ge(s_bias_cut, 7)
            for k in range(3):
                act.dma_start(bias3[k:k + 1, :], bias_part[k]).then_inc(s_bias3, 16)
            act.wait_ge(s_bias3, 48)
            normalise_edges(0, 0)
            normalise_nodes(0, 0, 0)
            run(act, step)
            for m in (TILES - 2, TILES - 1):
                exps(m)
                keep_sums(m)


        @block.vector
        def _(dve):
            dve.memset(ones3[:, :], 1.0).then_inc(s_bias_cut, 1)
            dve.wait_ge(s_raw, 96)
            dve.tensor_scalar(table_f[:, 0, :], raw_dst[:, :], APART, None, ALU.mult).then_inc(s_scaled, 1)
            dve.tensor_tensor(falls[:, :], raw_dst[:, :], raw_next[:, :], ALU.is_gt).then_inc(s_falls, 1)
            dve.wait_ge(s_falls, 1)
            dve.tensor_reduce(out=row_falls[:, :], in_=falls[:, :], op=ALU.max, axis=AX.X).then_inc(s_falls, 1)
            dve.tensor_scalar(table_f[:, 1, :], raw_next[:, :], APART, None, ALU.mult)
            dve.wait_ge(s_falls_T, 1)
            dve.tensor_reduce(out=unsorted[:, :], in_=ps_falls, op=ALU.max, axis=AX.X).then_inc(s_flag, 1)
            dve.wait_ge(s_flag, 1)
            with dve.If(dve.value_load(unsorted[0:1, 0:1], min_val=0, max_val=1) > 0):
                dve.wait_ge(s_sort_in, 64)
                dve.wait_ge(s_number_row, 1)
                with dve.Fori(0, TILES) as t:
                    dve.tensor_copy(moved_src[:, :], src_col[:, bass.ds(t, 1)])
                    dve.tensor_copy(moved_edge[:, :], edge_col[:, bass.ds(t, 1)]).then_inc(s_mask, 1)
                    dve.tensor_copy(moved_dst[:, :], key_col[:, bass.ds(t, 1)]).then_inc(s_mask, 1)
                    dve.wait_ge(s_mask, t * 6 + 2)
                    dve.tensor_copy(count[:, :], moved_edge[:, :]).then_inc(s_mask, 1)
                    dve.tensor_scalar(mask_row, key_row, moved_dst[:, :], None, ALU.is_equal)\
                        .then_inc(s_mask, 1)
                    dve.wait_ge(s_mask, t * 6 + 4)
                    dve.scalar_tensor_tensor(out=mask_row, in0=number_row, scalar=count[:, :],
                                             in1=mask_row, op0=ALU.is_lt, op1=ALU.mult).then_inc(s_mask, 1)
                    dve.wait_ge(s_mask, t * 6 + 5)
                    dve.scalar_tensor_tensor(out=mask_row, in0=key_row, scalar=moved_dst[:, :],
                                             in1=mask_row, op0=ALU.is_lt, op1=ALU.add).then_inc(s_mask, 1)
                    dve.wait_ge(s_mask, t * 6 + 6)
                    dve.tensor_reduce(out=count[:, :], in_=mask_row, op=ALU.add, axis=AX.X)\
                        .then_inc(s_count, 1)
                    dve.wait_ge(s_count, t + 1)
                    dve.tensor_scalar(place[:, :], count[:, :], 1.0, None, ALU.add).then_inc(s_place, 1)
                    dve.wait_ge(s_moved, t * 48 + 48)
                dve.wait_ge(s_tab_in, 64)
            dve.wait_ge(s_iota, 1)
            dve.tensor_copy(table_f[:, 2, :], raw_src[:, :])
            dve.tensor_copy(table_f[:, 3, :], raw_edge[:, :]).then_inc(s_tab_f, 1)
            dve.wait_ge(s_tab_T, 1)
            cols = ps_tab[:, 0:4 * TILES].rearrange("p (k t) -> p k t", k=4)
            dve.memset(dst_col[:, 0:1], -APART)
            dve.tensor_copy(dst_col[:, 1:TILES + 1], cols[:, 0, :]).then_inc(s_same_next, 1)
            dve.tensor_copy(dst_next[:, :], cols[:, 1, :]).then_inc(s_same_next, 1)
            dve.tensor_copy(tile_rows[:, 0:TILES, 0], cols[:, 2, :]).then_inc(s_cols, 1)
            dve.tensor_scalar(tile_rows[:, 0:TILES, 1], cols[:, 0, :], 1 / APART, float(N - 1), ALU.mult, ALU.min)\
                .then_inc(s_cols, 1)
            dve.tensor_scalar(tile_rows[:, 0:TILES, 2], cols[:, 3, :], float(E - 1), None, ALU.min)\
                .then_inc(s_cols, 1)
            dve.wait_ge(s_same_next, 2)
            dve.tensor_tensor(same_next[:, :], dst_col[:, 1:TILES + 1], dst_next[:, :], ALU.is_equal)\
                .then_inc(s_same_next, 1)
            dve.wait_ge(s_same_next, 3)
            dve.scalar_tensor_tensor(out=dst_next[:, :], in0=same_next[:, :], scalar=SKIP * APART,
                                     in1=dst_col[:, 1:TILES + 1], op0=ALU.mult, op1=ALU.add)\
                .then_inc(s_same_next, 1)
            dve.wait_ge(s_same_next, 4)
            dve.tensor_scalar(scatter_rows[:, :], dst_next[:, :], 1 / APART, None, ALU.mult)\
                .then_inc(s_same_next, 1)
            dve.wait_ge(s_limit, 3)
            dve.scalar_tensor_tensor(out=over[:, :], in0=dst_col[:, 1:TILES + 1], scalar=1 / APART,
                                     in1=limit[:, :], op0=ALU.mult, op1=ALU.is_ge).then_inc(s_over, 1)
            dve.wait_ge(s_over, 1)
            dve.wait_ge(s_same_next, 5)
            dve.tensor_reduce(out=late[96:P, :], in_=over[96:P, :], op=ALU.max, axis=AX.X)\
                .then_inc(s_late, 1)
            dve.scalar_tensor_tensor(out=loop_rows[:, :], in0=over[:, :], scalar=float(SKIP),
                                     in1=scatter_rows[:, :], op0=ALU.mult, op1=ALU.add)\
                .then_inc(s_over, 1)
            dve.wait_ge(s_over, 2)
            dve.tensor_copy(tile_rows[:, SHIFT:TILES + SHIFT, 3], loop_rows[:, :]).then_inc(s_cols, 1)

            def low_of_hT(n):
                dve.wait_ge(s_hT_edge, n + 1)
                wait(dve, s_proj, n * 3)
                dve.tensor_tensor(hT_edge[1][:, :, :, :],
                                  ps_hT_edge[:, :].rearrange("a (t c p) -> a t c p", t=2, c=KC),
                                  hT_edge[0][:, :, :, :].bitcast(F32), ALU.subtract).then_inc(s_hT_low, 1)

            def low_of_node_hT(n, j):
                p, tiles = nodes(isinstance(n, int) and n == FULL)
                count = min(2, tiles - 2 * j)
                dve.wait_ge(s_hT, n * 2 + j + 1)
                wait(dve, s_mm, n * 2 + j - 1)
                dve.tensor_tensor(hT_low[j][:, 0:count, :, 0:p],
                                  ps_hT[:, :].rearrange("a (t c p) -> a t c p", t=2, c=KC)[:, 0:count, :, 0:p],
                                  hT[j][:, 0:count, :, 0:p].bitcast(F32), ALU.subtract)\
                    .then_inc(s_hT_low_nodes, 1)

            def statistics(n, i, u):
                p, tiles = nodes(isinstance(n, int) and n == FULL)
                dve.wait_ge(s_x[u], i * 16 + 16)
                for j in range(2):
                    dve.bn_stats(bn[0:p, 2 + j, :], x_in[u][0:p, j, :])
                dve.wait_ge(s_gath[u], i * 48 + 48)
                dve.bn_stats(bn[:, 0, :], x_src[u][:, :])
                dve.bn_stats(bn[:, 1, :], x_dst[u][:, :]).then_inc(s_bn, 1)

            def aggregate(n, u):
                dve.wait_ge(s_bn, n + 1)
                hold(dve)
                for j in range(JT):
                    done = dve.bn_aggr(stats[u][:, j, :], bn[:, j, :])
                done.then_inc(s_stats, 1)

            def shifts(n, u):
                dve.wait_ge(s_rstd, n + 1)
                dve.scalar_tensor_tensor(out=shift[u][:, :], in0=stats[u][:, :, 0], scalar=-1.0,
                                         in1=rstd[u][:, :], op0=ALU.mult, op1=ALU.mult)\
                    .then_inc(s_shift, 1)

            def y_add(n, i, u, j):
                p, tiles = nodes(isinstance(n, int) and n == FULL)
                count = min(2, tiles - 2 * j)
                dve.wait_ge(s_mm, n * 2 + j + 1)
                if j == 0:
                    dve.wait_ge(s_xbs, n + 1)
                    if not (isinstance(i, int) and i == 0):
                        dve.wait_ge(s_store[u], i * 16)
                dve.tensor_tensor(y_out[u][0:p, 2 * j:2 * j + count, :],
                                  ps_y[j][0:p, 0:count * D].rearrange("p (t d) -> p t d", d=D),
                                  x_bs[u][0:p, 2 * j:2 * j + count, :], ALU.add).then_inc(s_y, 1)

            def head_dim(ap):
                return ap.rearrange("p (h c) -> p h c", c=C)

            def keys_and_values(n, u):
                dve.wait_ge(s_proj, n * 3 + 2)
                dve.wait_ge(s_e, n + 1)
                wait(dve, s_qk, n)
                dve.tensor_tensor(k_sb[:, :], ps_kv[:, 0:D], e_sb[:, :], ALU.add).then_inc(s_k, 1)
                wait(dve, s_weighted, n - 1)
                dve.tensor_tensor(v_sb[u][:, :], ps_kv[:, D:2 * D], e_sb[:, :], ALU.add).then_inc(s_v, 1)

            def query_key(n):
                dve.wait_ge(s_k, n + 1)
                dve.tensor_tensor(qk[:, :], q_sb[:, :], k_sb[:, :], ALU.mult).then_inc(s_qk, 1)

            def scores(n, u):
                dve.wait_ge(s_qk, n + 1)
                dve.tensor_reduce(out=alpha[u][:, :], in_=head_dim(qk[:, :]), op=ALU.add, axis=AX.X)\
                    .then_inc(s_alpha, 1)

            def segments(n, i, u):
                dve.wait_ge(s_row[u], i * 16 + 16)
                row = dst_row[u]
                dve.tensor_scalar(carry_to[u][96:P, :], row[96:P, 1:P + 1], dst_col[96:P, bass.ds(n, 1)],
                                  last_row[96:P, :], ALU.is_equal, ALU.mult)
                dve.tensor_scalar(same[u][:, :], row[:, 1:P + 1], dst_col[:, bass.ds(n + 1, 1)], None,
                                  ALU.is_equal).then_inc(s_same, 1)

            def max_before(n, u):
                return 0.0 if isinstance(n, int) and n == 0 else run_max[1 - u][:, P - 1:P]

            def first_max(n, u):
                dve.wait_ge(s_break, n + 1)
                dve.wait_ge(s_alphaT, n + 1)
                dve.tensor_tensor_scan(run_max[u][:, :], breaks[u][:, 0:P], ps_alphaT, max_before(n, u),
                                       ALU.add, ALU.max).then_inc(s_run, 1)

            def back_max(n, u):
                dve.wait_ge(s_run, n + 1)
                dve.tensor_tensor_scan(seg_max[:, ::-1], breaks[u][:, P:0:-1], run_max[u][:, ::-1], NEG,
                                       ALU.add, ALU.max).then_inc(s_seg, 1)

            def rise_of(n, u):
                dve.wait_ge(s_seg, n + 1)
                dve.tensor_scalar(rise[:, :], seg_max[:, 0:1], max_before(n, u), 0.0, ALU.subtract, ALU.max)\
                    .then_inc(s_rise, 1)

            def reciprocals(m):
                dve.wait_ge(s_sums_sb, m + 1)
                dve.reciprocal(recip[:, :], sums_sb[:, :, C]).then_inc(s_recip, 1)

            def divide(m):
                dve.wait_ge(s_recip, m + 1)
                wait(dve, s_final, m)
                dve.tensor_tensor(head_dim(attn[:, :]), sums_sb[:, :, 0:C],
                                  recip[:, :].unsqueeze(2).to_broadcast([P, H, C]), ALU.mult)\
                    .then_inc(s_attn, 1)

            def add_attn(m):
                dve.wait_ge(s_attn, m + 1)
                dve.tensor_tensor(final[:, m, :], final[:, m, :], attn[:, :], ALU.add).then_inc(s_final, 1)

            def weigh(m, u):
                dve.wait_ge(s_exp, m + 1)
                dve.wait_ge(s_v, m + 1)
                dve.tensor_tensor(weighted[:, :, 0:C], head_dim(v_sb[u][:, :]),
                                  weighted[:, :, C:HD].to_broadcast([P, H, C]), ALU.mult)\
                    .then_inc(s_weighted, 1)

            def distance(m, u):
                dve.wait_ge(s_back, m + 1)
                dve.tensor_tensor(below[:, :], alpha[u][:, :], ps_seg_max, ALU.subtract)\
                    .then_inc(s_below, 1)

            def step(n, i, u):
                start = isinstance(n, int)
                last = start and n == TILES - 1
                back = i if u else i - 1
                ahead = i + 1 if u else i
                if not (start and n < 2):
                    distance(n - 2, u)
                if not (start and n < 1):
                    y_add(n - 1, back, 1 - u, 1)
                if not last:
                    statistics(n + 1, ahead, 1 - u)
                low_of_node_hT(n, 0)
                if not last:
                    aggregate(n + 1, 1 - u)
                if not (start and n < 2):
                    weigh(n - 2, u)
                dve.wait_ge(s_gath[u], i * 48 + 48)
                dve.wait_ge(s_q, n + 1)
                dve.tensor_tensor(final[:, n, :], ps_qs[:, D:2 * D], x_dst[u][:, :], ALU.add)\
                    .then_inc(s_part, 1)
                if not (start and n < 1):
                    segments(n - 1, back, 1 - u)
                keys_and_values(n, u)
                low_of_node_hT(n, 1)
                if not last:
                    shifts(n + 1, 1 - u)
                query_key(n)
                if not (start and n < 1):
                    first_max(n - 1, 1 - u)
                if not (start and n < 2):
                    reciprocals(n - 2)
                if not (start and n < 1):
                    back_max(n - 1, 1 - u)
                if not (start and n < 2):
                    divide(n - 2)
                if not (start and n < 1):
                    rise_of(n - 1, 1 - u)
                y_add(n, i, u, 0)
                scores(n, u)
                if not (start and n < 2):
                    add_attn(n - 2)
                if not last:
                    low_of_hT(n + 1)

            dve.wait_ge(s_bias_in, 64)
            dve.tensor_tensor(bias_row[:, D:2 * D], bias_row[:, D:2 * D], bs_row[:, :], ALU.add)\
                .then_inc(s_bias_cut, 1)
            dve.wait_ge(s_bias_cut, 2)
            for k in range(3):
                if k:
                    dve.wait_ge(s_bias_cut, 2 * k + 1)
                    dve.tensor_tensor(bias_row[:, :], bias_row[:, :], bias_part[k - 1], ALU.subtract)\
                        .then_inc(s_bias_cut, 1)
                    dve.wait_ge(s_bias_cut, 2 * k + 2)
                dve.tensor_copy(bias_part[k], bias_row[:, :]).then_inc(s_bias_cut, 1)
            statistics(0, 0, 0)
            aggregate(0, 0)
            for k, ((high, low), given) in enumerate(SPLITS):
                if k:
                    shifts(0, 0)
                dve.wait_ge(s_w_high, k + 1)
                dve.tensor_tensor(low[:, :, :], given, high[:, :, :].bitcast(F32), ALU.subtract)\
                    .then_inc(s_w_low, 1)
            low_of_hT(0)
            run(dve, step)
            distance(TILES - 2, 0)
            y_add(TILES - 1, TILES // 2 - 1, 1, 1)
            weigh(TILES - 2, 0)
            segments(TILES - 1, TILES // 2 - 1, 1)
            first_max(TILES - 1, 1)
            back_max(TILES - 1, 1)
            rise_of(TILES - 1, 1)
            reciprocals(TILES - 2)
            divide(TILES - 2)
            add_attn(TILES - 2)
            distance(TILES - 1, 1)
            weigh(TILES - 1, 1)
            reciprocals(TILES - 1)
            divide(TILES - 1)
            add_attn(TILES - 1)

            dve.wait_ge(s_late, 1)
            with dve.If(dve.value_load(late[P - 1:P, 0:1], min_val=0, max_val=1) > 0):
                dve.wait_ge(s_final, TILES)
                for u in range(2):
                    dve.wait_ge(s_store[u], 16 * (TILES // 2))

                def stage(i, k):
                    if not isinstance(i, int):
                        dve.wait_ge(s_scat[k], i * 16)
                    t = i * SLOTS + k
                    dve.tensor_copy(staged(k), final[:, t, :])
                    dve.tensor_copy(scatter_now[:, k:k + 1], scatter_rows[:, bass.ds(t, 1)])\
                        .then_inc(s_staged, 1)

                for k in range(SLOTS):
                    stage(0, k)
                with dve.Fori(1, TILES // SLOTS) as i:
                    for k in range(SLOTS):
                        stage(i, k)

        @block.tensor
        def _(pe):
            pe.wait_ge(s_const, 6)
            pe.wait_ge(s_falls, 2)
            pe.transpose(ps_falls, row_falls[:, :], ident[0:TILES, 0:TILES]).then_inc(s_falls_T, 1)
            pe.wait_ge(s_tab_f, 1)
            for k in range(4):
                done = pe.transpose(ps_tab[:, k * TILES:(k + 1) * TILES], table_f[:, k, :],
                                    ident[0:TILES, 0:TILES])
            done.then_inc(s_tab_T, 1)

            def chunk(c):
                return slice(c * P, (c + 1) * P)

            def edge_transposes(n, u):
                pe.wait_ge(s_norm, n * 3 + 1)
                wait(pe, s_hT_low, n)
                for k in range(2):
                    for c in range(KC):
                        at = (k * KC + c) * P
                        done = pe.transpose(ps_hT_edge[:, at:at + P], edge_normed[u][:, k, chunk(c)],
                                            ident[:, :])
                done.then_inc(s_edgeT, 1)

            def attr_transposes(n, i, u):
                pe.wait_ge(s_gath[u], i * 48 + 48)
                wait(pe, s_below, n - 1)
                wait(pe, s_fade, n - 1)
                for c in range(KC):
                    done = pe.transpose(ps_eT[:, c * P:(c + 1) * P], e_in[u][:, chunk(c)], ident[:, :])
                done.then_inc(s_eT, 1)

            def node_transposes(n, i, u, j):
                p, tiles = nodes(isinstance(n, int) and n == FULL)
                pe.wait_ge(s_norm, n * 3 + 2 + j)
                wait(pe, s_hT, n * 2 + j)
                wait(pe, s_hT_low_nodes, n * 2 + j)
                for k in range(min(2, tiles - 2 * j)):
                    for c in range(KC):
                        at = (k * KC + c) * P
                        done = pe.transpose(ps_hT[:, at:at + p], normed[u][0:p, 2 * j + k, chunk(c)],
                                            ident[0:p, 0:p])
                done.then_inc(s_nodeT, 1)

            def node_products(n, i, u, j, between=None):
                p, tiles = nodes(isinstance(n, int) and n == FULL)
                pe.wait_ge(s_hT, n * 2 + j + 1)
                wait(pe, s_y, n * 2 + j - 1)
                for k in range(min(2, tiles - 2 * j)):
                    if k and between:
                        between()
                    at = ps_y[j][0:p, k * D:(k + 1) * D]
                    for c in range(KC):
                        for part in range(2):
                            pe.matmul(at, hT[j][:, k, c, 0:p], w_qs[part][:, c, D:2 * D],
                                      start=c == 0 and part == 0, stop=False)
                    if k == 0:
                        pe.wait_ge(s_hT_low_nodes, n * 2 + j + 1)
                    for c in range(KC):
                        done = pe.matmul(at, hT_low[j][:, k, c, 0:p], w_qs[0][:, c, D:2 * D],
                                         start=False, stop=c == KC - 1)
                done.then_inc(s_mm, 1)

            def product(to, which, w, low_ready=None):
                high, low = (part[:, which, :, :] for part in hT_edge)
                for c in range(KC):
                    for part in range(2):
                        pe.matmul(to, high[:, c, :], w[part][:, c, :], start=c == 0 and part == 0,
                                  stop=False)
                if low_ready:
                    low_ready()
                for c in range(KC):
                    pe.matmul(to, low[:, c, :], w[0][:, c, :], start=False, stop=False)

            def project_dst(n):
                pe.wait_ge(s_hT_edge, n + 1)
                wait(pe, s_part, n)
                product(ps_qs[:, :], 1, w_qs, lambda: pe.wait_ge(s_hT_low, n + 1))
                pe.matmul(ps_qs[:, :], ones3[:, :], bias3[:, 0:2 * D], start=False, stop=True)\
                    .then_inc(s_proj, 1)

            def project_src(n):
                wait(pe, s_v, n)
                product(ps_kv[:, :], 0, w_kv)
                pe.matmul(ps_kv[:, 0:D], ones3[:, :], bias3[:, 2 * D:3 * D], start=False, stop=True)\
                    .then_inc(s_proj, 1)

            def project_attr(n):
                pe.wait_ge(s_eTs, n + 1)
                for c in range(KC):
                    done = pe.matmul(ps_ev, eT[:, c, :], w_e[:, c, :], start=c == 0, stop=c == KC - 1)
                done.then_inc(s_proj, 1)

            def segment_sums(m, u):
                pe.wait_ge(s_weighted, m + 1)
                pe.wait_ge(s_carried, m + 1)
                pe.wait_ge(s_same, m + 1)
                wait(pe, s_sums_sb, m)
                flat = "p h c -> p (h c)"
                pe.matmul(ps_sums, same[u][:, :], weighted[:, :, :].rearrange(flat), start=True, stop=False)
                pe.matmul(ps_sums, carry_to[u][96:P, :], carried[96:P, :, :].rearrange(flat),
                          start=False, stop=True).then_inc(s_sums, 1)

            def turn_scores(m, u):
                pe.wait_ge(s_alpha, m + 1)
                pe.transpose(ps_alphaT, alpha[u][:, :], ident[:, :]).then_inc(s_alphaT, 1)

            def turn_maxima(m):
                pe.wait_ge(s_rise, m + 1)
                hold(pe)
                pe.transpose(ps_seg_max, seg_max[:, :], ident[0:H, 0:H])
                pe.matmul(ps_rise, rise[:, 0:1].to_broadcast([H, P]), ident[0:H, 0:H],
                          start=True, stop=True).then_inc(s_back, 1)

            def step(n, i, u):
                start = isinstance(n, int)
                node_transposes(n, i, u, 0)
                project_dst(n)
                attr_transposes(n, i, u)
                project_src(n)
                project_attr(n)
                node_transposes(n, i, u, 1)
                if not (start and n < 2):
                    segment_sums(n - 2, u)
                if not (start and n < 1):
                    pe.wait_ge(s_e, n + 1)
                    turn_scores(n - 1, 1 - u)
                node_products(n, i, u, 0)
                last = start and n == TILES - 1
                node_products(n, i, u, 1, None if last else lambda: edge_transposes(n + 1, 1 - u))
                if not (start and n < 1):
                    turn_maxima(n - 1)

            edge_transposes(0, 0)
            pe.wait_ge(s_weights, 16 * 5 * KC)
            pe.wait_ge(s_w_low, 2)
            pe.wait_ge(s_bias3, 48)
            pe.wait_ge(s_cols, 4)
            run(pe, step)
            segment_sums(TILES - 2, 0)
            pe.wait_ge(s_below, TILES - 1)
            pe.wait_ge(s_fade, TILES - 1)
            turn_scores(TILES - 1, 1)
            turn_maxima(TILES - 1)
            segment_sums(TILES - 1, 1)


_INS = ["x", "src", "dst", "edge_attr_256", "L0_gnn_Wq", "L0_gnn_bq", "L0_gnn_Wk", "L0_gnn_bk",
        "L0_gnn_Wv", "L0_gnn_bv", "L0_gnn_We", "L0_gnn_Ws", "L0_gnn_bs"]


def kernel(**inputs):
    import numpy as _np
    import concourse.bacc as _bacc
    from concourse import mybir as _mybir
    from concourse.bass_utils import run_bass_kernel_spmd as _run

    nc = _bacc.Bacc("TRN2", target_bir_lowering=False, num_devices=1)
    arrays, args = {}, []
    for name in _INS:
        a = _np.ascontiguousarray(inputs[name])
        arrays[f"in_{name}"] = a
        args.append(nc.dram_tensor(f"in_{name}", a.shape, _mybir.dt.from_np(a.dtype), kind="ExternalInput").ap())
    args.append(nc.dram_tensor("out_rows", inputs["x"].shape, _mybir.dt.float32, kind="ExternalOutput").ap())
    build(nc, *args)
    r = _run(nc, [arrays], core_ids=[0])
    return r.results[0]["out_rows"]
```
